# Optimizing a Trainium2 kernel written in Bass

```python
import numpy as np
import jax
import jax.numpy as jnp

def _softmax(x, axis=-1):
    return jax.nn.softmax(x, axis=axis)

def _gelu(x):
    return jax.nn.gelu(x, approximate=True)

def _silu(x):
    return jax.nn.silu(x)

def _sigmoid(x):
    return jax.nn.sigmoid(x)

def _layernorm(x, axis=-1, eps=1e-05):
    m = jnp.mean(x, axis=axis, keepdims=True)
    v = jnp.var(x, axis=axis, keepdims=True)
    return (x - m) / jnp.sqrt(v + eps)

def _scatter_add(tgt, idx, src, axis=0):
    return tgt.at[idx].add(src)

def _segment_sum(src, seg, n):
    return jax.ops.segment_sum(src, seg, n)
kernel_name = 'mk_seq_preln_d1_jaxref_r8_5d7cf7'

def setup_inputs(seed: int=0):
    np.random.seed(seed)
    _w = jnp.asarray

    def _L0_attn_setup():
        import jax, jax.numpy as jnp
        import numpy as np
        B, S, D = (4, 512, 128)
        H = 8
        DK = D // H
        DV = D // H
        KLEPE = 5
        ROPE_BASE = 10000.0

        def rotate_half(x):
            x1, x2 = jnp.split(x, 2, axis=-1)
            return jnp.concatenate([-x2, x1], axis=-1)

        def rope_sin_cos(seq_len, dim):
            inv_freq = 1.0 / ROPE_BASE ** (jnp.arange(0, dim, 2, dtype=jnp.float32) / dim)
            freqs = jnp.arange(seq_len, dtype=jnp.float32)[:, None] * inv_freq[None, :]
            emb = jnp.concatenate([freqs, freqs], axis=-1)
            return (jnp.sin(emb), jnp.cos(emb))

        def mala_attn(q, k, v):
            sin, cos = rope_sin_cos(q.shape[1], q.shape[-1])
            sin, cos = (sin[None, :, None, :], cos[None, :, None, :])
            q = q * cos + rotate_half(q) * sin
            k = k * cos + rotate_half(k) * sin
            scale = q.shape[-1] ** (-0.5)
            seq_len = q.shape[1]
            kv = jnp.einsum('bshd,bshe->bhde', k, v)
            ksum = k.sum(axis=1)
            vsum = v.sum(axis=1)
            num = jnp.einsum('bshd,bhde->bshe', q, kv) * scale + vsum[:, None, :, :]
            den = jnp.einsum('bshd,bhd->bsh', q, ksum) * scale + seq_len
            return num / den[..., None]

        def lepe_conv(v, w, b):
            Bb, Ss = (v.shape[0], v.shape[1])
            x = v.transpose(0, 2, 3, 1).reshape(Bb, H * DV, Ss)
            y = jax.lax.conv_general_dilated(x, w, window_strides=(1,), padding=[(KLEPE // 2, KLEPE // 2)], dimension_numbers=('NCH', 'OIH', 'NCH'), feature_group_count=H * DV)
            y = y + b[None, :, None]
            return y.reshape(Bb, H, DV, Ss).transpose(0, 3, 1, 2)
        key = jax.random.key(seed)
        ks = jax.random.split(key, 8)
        w = 0.02
        return {'hidden_states': jax.random.normal(ks[0], (B, S, D), dtype=jnp.float32), 'Wq': jax.random.normal(ks[1], (D, D), dtype=jnp.float32) * w, 'Wk': jax.random.normal(ks[2], (D, D), dtype=jnp.float32) * w, 'Wv': jax.random.normal(ks[3], (D, D), dtype=jnp.float32) * w, 'Wg': jax.random.normal(ks[4], (D, D), dtype=jnp.float32) * w, 'Wo': jax.random.normal(ks[5], (D, D), dtype=jnp.float32) * w, 'lepe_w': jax.random.normal(ks[6], (D, 1, KLEPE), dtype=jnp.float32) * 0.1, 'lepe_b': jnp.zeros((D,), dtype=jnp.float32)}
    _L0_attn_in = _L0_attn_setup()

    def _L0_ffn_setup():
        import jax, jax.numpy as jnp
        import numpy as np
        FEATURES = 128
        D_IN = 128

        def fp8_gemm_optimized(x, input_scale, kernel, kernel_scale):
            s_in = input_scale[0]
            s_k = kernel_scale[0]
            x_q = (x.astype(jnp.float32) / s_in).astype(jnp.float8_e4m3fn)
            k_q = (kernel.astype(jnp.float32) / s_k).astype(jnp.float8_e4m3fn)
            y = jnp.dot(x_q.astype(jnp.float32), k_q.astype(jnp.float32), preferred_element_type=jnp.float32)
            return y * (s_in * s_k)
        key = jax.random.key(seed)
        kx, kk, kb = jax.random.split(key, 3)
        x = jax.random.normal(kx, (4, 1024, D_IN), dtype=jnp.float32)
        limit = np.sqrt(6.0 / (D_IN + FEATURES)).astype(np.float32)
        kernel = jax.random.uniform(kk, (D_IN, FEATURES), dtype=jnp.float32, minval=-limit, maxval=limit).astype(jnp.bfloat16)
        input_scale = jnp.ones((1,), dtype=jnp.float32)
        kernel_scale = jnp.ones((1,), dtype=jnp.float32)
        bias = jnp.zeros((FEATURES,), dtype=jnp.bfloat16)
        return {'x': x, 'kernel': kernel, 'input_scale': input_scale, 'kernel_scale': kernel_scale, 'bias': bias}
    _L0_ffn_in = _L0_ffn_setup()
    _d = {'L0_attn_hidden_states': _L0_attn_in['hidden_states'], 'L0_attn_Wq': _L0_attn_in['Wq'], 'L0_attn_Wk': _L0_attn_in['Wk'], 'L0_attn_Wv': _L0_attn_in['Wv'], 'L0_attn_Wg': _L0_attn_in['Wg'], 'L0_attn_Wo': _L0_attn_in['Wo'], 'L0_attn_lepe_w': _L0_attn_in['lepe_w'], 'L0_attn_lepe_b': _L0_attn_in['lepe_b'], 'L0_ffn_kernel': _L0_ffn_in['kernel'], 'L0_ffn_input_scale': _L0_ffn_in['input_scale'], 'L0_ffn_kernel_scale': _L0_ffn_in['kernel_scale'], 'L0_ffn_bias': _L0_ffn_in['bias']}
    _x0 = _d['L0_attn_hidden_states']
    _d['L0_attn_hidden_states'] = jax.random.normal(jax.random.fold_in(jax.random.key(seed), 1), (32, 256, 128), dtype=_x0.dtype)
    del _x0
    return _d

def reference(L0_attn_hidden_states, L0_attn_Wq, L0_attn_Wk, L0_attn_Wv, L0_attn_Wg, L0_attn_Wo, L0_attn_lepe_w, L0_attn_lepe_b, L0_ffn_kernel, L0_ffn_input_scale, L0_ffn_kernel_scale, L0_ffn_bias):

    def _L0_attn_ref(hidden_states, Wq, Wk, Wv, Wg, Wo, lepe_w, lepe_b):
        import jax, jax.numpy as jnp
        import numpy as np
        B, S, D = (4, 512, 128)
        H = 8
        DK = D // H
        DV = D // H
        KLEPE = 5
        ROPE_BASE = 10000.0

        def rotate_half(x):
            x1, x2 = jnp.split(x, 2, axis=-1)
            return jnp.concatenate([-x2, x1], axis=-1)

        def rope_sin_cos(seq_len, dim):
            inv_freq = 1.0 / ROPE_BASE ** (jnp.arange(0, dim, 2, dtype=jnp.float32) / dim)
            freqs = jnp.arange(seq_len, dtype=jnp.float32)[:, None] * inv_freq[None, :]
            emb = jnp.concatenate([freqs, freqs], axis=-1)
            return (jnp.sin(emb), jnp.cos(emb))

        def mala_attn(q, k, v):
            sin, cos = rope_sin_cos(q.shape[1], q.shape[-1])
            sin, cos = (sin[None, :, None, :], cos[None, :, None, :])
            q = q * cos + rotate_half(q) * sin
            k = k * cos + rotate_half(k) * sin
            scale = q.shape[-1] ** (-0.5)
            seq_len = q.shape[1]
            kv = jnp.einsum('bshd,bshe->bhde', k, v)
            ksum = k.sum(axis=1)
            vsum = v.sum(axis=1)
            num = jnp.einsum('bshd,bhde->bshe', q, kv) * scale + vsum[:, None, :, :]
            den = jnp.einsum('bshd,bhd->bsh', q, ksum) * scale + seq_len
            return num / den[..., None]

        def lepe_conv(v, w, b):
            Bb, Ss = (v.shape[0], v.shape[1])
            x = v.transpose(0, 2, 3, 1).reshape(Bb, H * DV, Ss)
            y = jax.lax.conv_general_dilated(x, w, window_strides=(1,), padding=[(KLEPE // 2, KLEPE // 2)], dimension_numbers=('NCH', 'OIH', 'NCH'), feature_group_count=H * DV)
            y = y + b[None, :, None]
            return y.reshape(Bb, H, DV, Ss).transpose(0, 3, 1, 2)
        Bb, Ss, _ = hidden_states.shape
        q = (hidden_states @ Wq.T).reshape(Bb, Ss, H, DK)
        k = (hidden_states @ Wk.T).reshape(Bb, Ss, H, DK)
        v = (hidden_states @ Wv.T).reshape(Bb, Ss, H, DV)
        o_gate = hidden_states @ Wg.T
        o = mala_attn(q, k, v) + lepe_conv(v, lepe_w, lepe_b)
        o = o.reshape(Bb, Ss, H * DV) * o_gate
        return o @ Wo.T

    def _L0_ffn_ref(x, kernel, input_scale, kernel_scale, bias):
        import jax, jax.numpy as jnp
        import numpy as np
        FEATURES = 128
        D_IN = 128

        def fp8_gemm_optimized(x, input_scale, kernel, kernel_scale):
            s_in = input_scale[0]
            s_k = kernel_scale[0]
            x_q = (x.astype(jnp.float32) / s_in).astype(jnp.float8_e4m3fn)
            k_q = (kernel.astype(jnp.float32) / s_k).astype(jnp.float8_e4m3fn)
            y = jnp.dot(x_q.astype(jnp.float32), k_q.astype(jnp.float32), preferred_element_type=jnp.float32)
            return y * (s_in * s_k)
        dtype = jnp.bfloat16
        x = x.astype(dtype)
        orig_shape = x.shape
        x2 = x.reshape(-1, x.shape[-1])
        y = fp8_gemm_optimized(x2, input_scale, kernel, kernel_scale)
        y = y.astype(dtype) + bias
        return y.reshape(orig_shape[:-1] + (FEATURES,))
    x = L0_attn_hidden_states
    x = x + _L0_attn_ref(_layernorm(x, axis=-1), L0_attn_Wq, L0_attn_Wk, L0_attn_Wv, L0_attn_Wg, L0_attn_Wo, L0_attn_lepe_w, L0_attn_lepe_b)
    x = x + _L0_ffn_ref(_layernorm(x, axis=-1), L0_ffn_kernel, L0_ffn_input_scale, L0_ffn_kernel_scale, L0_ffn_bias)
    return x

_drawn_inputs = setup_inputs


def setup_inputs(seed=0):
    import zlib

    import numpy as np

    out = dict(_drawn_inputs(seed))
    spreads = {'L0_attn_lepe_b': (0.0, 0.627), 'L0_ffn_bias': (0.0, 0.326)}
    factors = {'L0_attn_Wq': 8.0,
     'L0_attn_Wk': 8.0,
     'L0_attn_Wv': 7.325,
     'L0_attn_Wg': 4.822,
     'L0_attn_Wo': 4.924,
     'L0_attn_lepe_w': 7.301}
    for name, (base, spread) in spreads.items():
        noise = np.random.default_rng([zlib.crc32(name.encode()), seed]).standard_normal(out[name].shape)
        drawn = base * np.exp(spread * noise) if base else spread * noise
        out[name] = jnp.asarray(drawn.astype(out[name].dtype))
    for name, factor in factors.items():
        out[name] = (out[name] * factor).astype(out[name].dtype)
    return out
```

```python
from collections import namedtuple
from contextlib import ExitStack

import concourse.bass as bass
from concourse import mybir

P = 128
D = 128
B, S = 32, 256
H, DK = 8, 16
HALF = DK // 2
TAPS = 5
EPS = 1e-5
ROPE_BASE = 10000.0

TPB = S // P
BPU = 2
TPU = TPB * BPU
U = B // BPU
W = TPU * P
DEN = H
NW = D + DEN
LAG = 3
UNROLL = 4

F32 = mybir.dt.float32
BF16 = mybir.dt.bfloat16
F8 = mybir.dt.float8e4
I32 = mybir.dt.int32
ALU = mybir.AluOpType
ACT = mybir.ActivationFunctionType

Unit = namedtuple("Unit", "n r")


def unit(step, back):
    return Unit(step.n - back, (step.r - back) % UNROLL)


def live(u):
    return not isinstance(u.n, int) or 0 <= u.n < U


def begun(u, back):
    return not isinstance(u.n, int) or u.n >= back


def count(u, back=0):
    n = u.n - back
    return min(n, U - 1) + 1 if isinstance(n, int) else n + 1


def run_steps(eng, step):
    for t in range(UNROLL):
        step(Unit(t, t % UNROLL))
    with eng.Fori(UNROLL, U, UNROLL) as i:
        for k in range(UNROLL):
            step(Unit(i + k, k))
    for t in range(U, U + LAG):
        step(Unit(t, t % UNROLL))


def build(nc, x, wq, wk, wv, wg, wo, lepe_w, lepe_b, ffn_w, s_in, s_k, ffn_b,
          cos_c, sin_c, ident_c, mask_c, hmask_c, sel_c, vrow_c, out):
    ctx = ExitStack()
    with ctx:
        def sb(name, shape, dt=F32):
            return ctx.enter_context(nc.sbuf_tensor(name, shape, dt))

        def ps(name, shape):
            return ctx.enter_context(nc.psum_tensor(name, shape, F32))

        def sem(name):
            return ctx.enter_context(nc.semaphore(name))

        cos_t = sb("cos_t", [P, TPB, 2 * D])
        sin_t = sb("sin_t", [P, TPB, 2 * D])
        ident = sb("ident", [P, P])
        identb = sb("identb", [P, P], BF16)
        mask = sb("mask", [P, D])
        hmask = sb("hmask", [P, H])
        sel = sb("sel", [3 * BPU, BPU, P], BF16)
        sel_f = sb("sel_f", [3 * BPU, BPU, P])
        vrow_f = sb("vrow_f", [3 * BPU, NW])
        w_raw = sb("w_raw", [P, 5, D])
        w_qk = sb("w_qk", [P, 2, 2, D // 2])
        w_gv = sb("w_gv", [P, 2, D])
        w_o = sb("w_o", [P, D])
        conv_w = sb("conv_w", [P, TAPS])
        conv_b = sb("conv_b", [P, 1])
        fw = sb("fw", [P, D], BF16)
        fwq = sb("fwq", [P, D], BF16)
        fb = sb("fb", [P, D], BF16)
        sc = sb("sc", [P, 2])
        rsc = sb("rsc", [P, 2])
        ysc = sb("ysc", [P, 1])
        small = sb("small", [P, 2], I32)
        qv = sb("qv", [P, W])
        qe = sb("qe", [P, W])
        qr = sb("qr", [P, W])
        qn = sb("qn", [P, W])
        mhalf = sb("mhalf", [P, TPU])

        xs = sb("xs", [P, UNROLL, TPU, D])
        st1 = sb("st1", [P, 2, TPU, 6])
        mv1 = sb("mv1", [P, 2, TPU, 2])
        nm1 = sb("nm1", [P, 2, TPU])
        ve1 = sb("ve1", [P, 2, TPU])
        rs1 = sb("rs1", [P, 2, TPU])
        h = sb("h", [P, 2, TPU, D])
        hT = sb("hT", [P, 2, W])
        rc = sb("rc", [P, BPU, TPB, 2, D])
        rs = sb("rs", [P, BPU, TPB, 2, D])
        qk = sb("qk", [P, 2, BPU, 2, TPB * 2, D // 2])
        gv = sb("gv", [P, UNROLL, TPU, 2 * D + 1])
        qT = sb("qT", [P, 2, W])
        vT = sb("vT", [P, 2, BPU, S])
        vsum = sb("vsum", [P, 2, BPU])
        vres = sb("vres", [P, 2, BPU])
        vsp = sb("vsp", [P, 2, BPU, 3], BF16)
        vrow = sb("vrow", [3 * BPU, 2, NW], BF16)
        kvs = sb("kvs", [P, 2, BPU, NW])
        acc = sb("acc", [P, 2, BPU, S])
        rden = sb("rden", [P, TPU, H])
        t1 = sb("t1", [P, TPU, D])
        t2 = sb("t2", [P, 2, TPU, D])
        o = sb("o", [P, 2, TPU, D])
        oT = sb("oT", [P, 2, W])
        x2 = sb("x2", [P, 2, TPU, D])
        st2 = sb("st2", [P, 2, TPU, 6])
        mv2 = sb("mv2", [P, 2, TPU, 2])
        nm2 = sb("nm2", [P, 2, TPU])
        ve2 = sb("ve2", [P, 2, TPU])
        rs2 = sb("rs2", [P, 2, TPU])
        h2 = sb("h2", [P, 2, TPU, D], BF16)
        q8 = sb("q8", [P, 2, W], F8)
        q16 = sb("q16", [P, W], BF16)
        yb = sb("yb", [P, 2, TPU, D], BF16)
        yc = sb("yc", [P, 2, TPU, D], BF16)
        ob = sb("ob", [P, 2, TPU, D])

        p_qk = [ps(f"p_qk{j}", [P, TPB, 2, D]) for j in range(BPU)]
        p_gv = [ps(f"p_gv{j}", [P, TPB, 2 * D]) for j in range(BPU)]
        p_num = ps("p_num", [P, TPU, 2 * D])
        p_lepe = ps("p_lepe", [P, TPU, D])
        p_t = ps("p_t", [P, W])
        p_vT = p_gv[0][:, :, :].rearrange("p a d -> p (a d)").rearrange("p (j s) -> p j s", j=BPU)
        p_vrow = p_gv[0][0:3 * BPU, 0, 0:D]
        p_oT = p_gv[1][:, :, :].rearrange("p a d -> p (a d)")
        p_y = p_oT
        p_kv = p_num[:, 0:2, :]
        p_proj = p_num[:, 2:4, :].rearrange("p t d -> p (t d)").rearrange("p (t d) -> p t d", t=TPU)
        p_h2T = p_t[:, 0:W // 2].bitcast(BF16)

        x_in = [sem(f"x_in{r}") for r in range(UNROLL)]
        c_in = sem("c_in")
        out_done = [sem(f"out_done{r}") for r in range(2)]
        setup_pe = sem("setup_pe")
        setup_dve = sem("setup_dve")
        w_ready = sem("w_ready")
        rounding = [sem(f"rounding{n}") for n in range(N_ROUNDING)]
        w_chain = sem("w_chain")
        const_set = sem("const_set")
        stats1_done = sem("stats1_done")
        aggr1_done = sem("aggr1_done")
        nm1_done = sem("nm1_done")
        rstd1_done = sem("rstd1_done")
        h_done = sem("h_done")
        hT_filled = sem("hT_filled")
        hT_done = sem("hT_done")
        qk_filled = [sem(f"qk_filled{j}") for j in range(BPU)]
        gv_filled = [sem(f"gv_filled{j}") for j in range(BPU)]
        gv_done = [sem(f"gv_done{j}") for j in range(BPU)]
        rope_done = [sem(f"rope_done{j}") for j in range(BPU)]
        qk_done = [sem(f"qk_done{j}") for j in range(BPU)]
        vT_filled = sem("vT_filled")
        vT_done = sem("vT_done")
        tap0_done = sem("tap0_done")
        conv_done = [sem(f"conv_done{j}") for j in range(TAPS - 1)]
        vsp1 = sem("vsp1")
        vsp2 = sem("vsp2")
        vsp_done = sem("vsp_done")
        vrow_filled = sem("vrow_filled")
        vrow_done = sem("vrow_done")
        qT_filled = sem("qT_filled")
        qT_done = sem("qT_done")
        kv_filled = sem("kv_filled")
        kvs_done = sem("kvs_done")
        num_filled = sem("num_filled")
        rden_done = sem("rden_done")
        t1_done = sem("t1_done")
        lepe_filled = sem("lepe_filled")
        t2_done = sem("t2_done")
        o_done = sem("o_done")
        oT_filled = sem("oT_filled")
        oT_done = sem("oT_done")
        proj_filled = sem("proj_filled")
        x2_done = sem("x2_done")
        stats2_done = sem("stats2_done")
        aggr2_done = sem("aggr2_done")
        nm2_done = sem("nm2_done")
        rstd2_done = sem("rstd2_done")
        h2_done = sem("h2_done")
        h2T_filled = sem("h2T_filled")
        q8_done = sem("q8_done")
        y_filled = sem("y_filled")
        yb_done = sem("yb_done")
        yc_done = sem("yc_done")
        ob_done = sem("ob_done")

        x_v = x.rearrange("(u j) (a p) d -> u p (j a) d", j=BPU, p=P)
        out_v = out.rearrange("(u j) (a p) d -> u p (j a) d", j=BPU, p=P)
        block = ctx.enter_context(nc.Block())

        @block.sync
        def _(sp):
            def load_x(u):
                if begun(u, UNROLL):
                    sp.wait_ge(x2_done, count(u, UNROLL))
                sp.dma_start(xs[:, u.r], x_v[u.n]).then_inc(x_in[u.r], 16)

            def store(u):
                if not live(u):
                    return
                sp.wait_ge(ob_done, count(u))
                sp.dma_start(out_v[u.n], ob[:, u.r % 2]).then_inc(out_done[u.r % 2], 16)

            load_x(Unit(0, 0))

            def step(t):
                nxt = unit(t, -1)
                if live(nxt):
                    load_x(nxt)
                if live(unit(t, 3)):
                    store(unit(t, 3))

            for t in range(UNROLL):
                step(Unit(t, t))
            with sp.Fori(UNROLL, U - UNROLL, UNROLL) as i:
                for k in range(UNROLL):
                    step(Unit(i + k, k))
            for t in range(U - UNROLL, U + LAG):
                step(Unit(t, t % UNROLL))
            for r in range(2):
                sp.wait_ge(out_done[r], 16 * (U // 2))

        @block.scalar
        def _(act):
            loads = [(w_raw[:, n], w) for n, w in enumerate((wq, wk, wv, wg, wo))]
            loads += [(ident[:], ident_c), (cos_t[:], cos_c), (sin_t[:], sin_c),
                      (mask[:], mask_c), (hmask[:], hmask_c), (sel_f[:], sel_c), (vrow_f[:], vrow_c),
                      (conv_w[:], lepe_w.rearrange("c a k -> c (a k)")),
                      (conv_b[:], lepe_b.rearrange("(c a) -> c a", a=1)), (fw[:], ffn_w),
                      (fb[:], ffn_b.rearrange("(a c) -> a c", a=1).broadcast_to([P, D])),
                      (sc[:, 0:1], s_in.rearrange("(a c) -> a c", a=1).broadcast_to([P, 1])),
                      (sc[:, 1:2], s_k.rearrange("(a c) -> a c", a=1).broadcast_to([P, 1]))]
            for dst, src in loads:
                act.dma_start(dst, src).then_inc(c_in, 16)
            assert len(loads) == N_LOADS
            act.wait_ge(c_in, 16 * N_LOADS)

            def quantise(u):
                act.wait_ge(h2T_filled, count(u))
                if begun(u, 2):
                    act.wait_ge(y_filled, count(u, 2))
                act.nop(nofuse=True)
                nc.scalar.activation(q8[:, u.r % 2], p_h2T, ACT.Copy, scale=rsc[:, 0:1],
                                     saturate=False).then_inc(q8_done, 1)

            def quantise_if_small(u):
                if not live(u):
                    return
                with act.If(is_small == 1):
                    quantise(u)

            def move_vT(u):
                if not live(u):
                    return
                act.wait_ge(vT_filled, count(u))
                if begun(u, 2):
                    act.wait_ge(vsp_done, count(u, 2))
                if begun(u, 2):
                    act.wait_ge(conv_done[-1], count(u, 2))
                for j in range(BPU):
                    last = nc.scalar.activation(vT[:, u.r % 2, j], p_vT[:, j], ACT.Copy,
                                                accum_out=vsum[:, u.r % 2, j:j + 1])
                last.then_inc(vT_done, 1)
                if begun(u, 2):
                    act.wait_ge(lepe_filled, count(u, 2))
                nc.scalar.activation(acc[:, u.r % 2], p_vT, ACT.Identity, scale=conv_w[:, TAPS // 2:TAPS // 2 + 1],
                                     bias=conv_b[:, 0:1]).then_inc(tap0_done, 1)

            def move_y(u):
                if not live(u):
                    return
                act.wait_ge(y_filled, count(u))
                if begun(u, 2):
                    act.wait_ge(yc_done, count(u, 2))
                nc.scalar.activation(yb[:, u.r % 2], p_y.rearrange("p (t d) -> p t d", t=TPU), ACT.Copy,
                                     scale=ysc[:, 0:1]).then_inc(yb_done, 1)

            def move_qT(u):
                if not live(u):
                    return
                act.wait_ge(qT_filled, count(u))
                if begun(u, 2):
                    act.wait_ge(num_filled, count(u, 2))
                nc.scalar.activation(qT[:, u.r % 2], p_t[:], ACT.Copy).then_inc(qT_done, 1)

            def move_vrow(u):
                if not live(u):
                    return
                act.wait_ge(vrow_filled, count(u))
                nc.scalar.activation(vrow[:, u.r % 2, 0:D], p_vrow, ACT.Copy).then_inc(vrow_done, 1)

            def move_oT(u):
                if not live(u):
                    return
                act.wait_ge(oT_filled, count(u))
                if begun(u, 2):
                    act.wait_ge(proj_filled, count(u, 2))
                nc.scalar.activation(oT[:, u.r % 2], p_oT, ACT.Copy).then_inc(oT_done, 1)

            def move_hT(u):
                if not live(u):
                    return
                act.wait_ge(hT_filled, count(u))
                if begun(u, 2):
                    act.wait_ge(gv_filled[-1], count(u, 2))
                nc.scalar.activation(hT[:, u.r % 2], p_t[:], ACT.Copy).then_inc(hT_done, 1)

            def move_gv(u):
                if not live(u):
                    return
                if begun(u, UNROLL):
                    act.wait_ge(o_done, count(u, UNROLL))
                for j in range(BPU):
                    act.wait_ge(gv_filled[j], count(u))
                    nc.scalar.activation(gv[:, u.r, TPB * j:TPB * (j + 1), 0:2 * D], p_gv[j][:],
                                         ACT.Copy).then_inc(gv_done[j], 1)

            def step(t):
                quantise_if_small(unit(t, 3))
                move_vT(unit(t, 1))
                move_y(unit(t, 3))
                move_qT(unit(t, 1))
                move_vrow(unit(t, 1))
                move_oT(unit(t, 2))
                move_hT(unit(t, 0))
                move_gv(unit(t, 0))

            act.wait_ge(w_ready, 1)
            is_small = act.value_load(small[0:1, 0:1], min_val=0, max_val=1)
            run_steps(act, step)

        @block.gpsimd
        def _(pool):
            nc.gpsimd.memset(mhalf[:], -0.5).then_inc(const_set, 1)
            nc.gpsimd.memset(gv[:, :, :, 2 * D:2 * D + 1], 1.0).then_inc(const_set, 1)
            pool.wait_ge(const_set, 2)

            def add_rope(u):
                if not live(u):
                    return
                for j in range(BPU):
                    pool.wait_ge(rope_done[j], count(u))
                    if begun(u, 2):
                        pool.wait_ge(kv_filled, count(u, 2))
                    nc.gpsimd.tensor_tensor(
                        qk[:, u.r % 2, j].rearrange("p q t d -> p t q d"),
                        rc[:, j].rearrange("p a h (q d) -> p (a h) q d", q=2),
                        rs[:, j].rearrange("p a h (q d) -> p (a h) q d", q=2), ALU.add).then_inc(qk_done[j], 1)

            def gate(u):
                if not live(u):
                    return
                pool.wait_ge(t2_done, count(u))
                if begun(u, 2):
                    pool.wait_ge(oT_filled, count(u, 2))
                nc.gpsimd.tensor_tensor(o[:, u.r % 2], t2[:, u.r % 2], gv[:, u.r, :, 0:D],
                                        ALU.mult).then_inc(o_done, 1)

            def split_vsum(u):
                if not live(u):
                    return
                s = u.r % 2
                pool.wait_ge(vT_done, count(u))
                if begun(u, 2):
                    pool.wait_ge(vrow_filled, count(u, 2))
                pool.nop(nofuse=True)
                nc.gpsimd.tensor_scalar(vsp[:, s, :, 0], vsum[:, s], 1.0, 0.0, ALU.mult,
                                        ALU.add).then_inc(vsp1, 1)
                pool.wait_ge(vsp1, count(u))
                nc.gpsimd.tensor_tensor(vres[:, s], vsum[:, s], vsp[:, s, :, 0], ALU.subtract)
                nc.gpsimd.tensor_tensor(vsp[:, s, :, 1], vsum[:, s], vsp[:, s, :, 0],
                                        ALU.subtract).then_inc(vsp2, 1)
                pool.wait_ge(vsp2, count(u))
                nc.gpsimd.tensor_tensor(vsp[:, s, :, 2], vres[:, s], vsp[:, s, :, 1],
                                        ALU.subtract).then_inc(vsp_done, 1)

            def norm(u, src, dst, mv, nm, ve, rst, aggr_done, nm_done, rstd_done, done):
                s = u.r % 2
                pool.wait_ge(aggr_done, count(u))
                pool.nop(nofuse=True)
                nc.gpsimd.tensor_scalar(ve[:, s], mv[:, s, :, 1], 1.0, EPS, ALU.mult, ALU.add)
                nc.gpsimd.tensor_scalar(nm[:, s], mv[:, s, :, 0], -1.0, 0.0, ALU.mult, ALU.add).then_inc(nm_done, 1)
                pool.wait_ge(nm_done, count(u))
                nc.gpsimd.tensor_tensor(rst[:, s], ve[:, s], mhalf[:], ALU.pow).then_inc(rstd_done, 1)
                pool.wait_ge(rstd_done, count(u))
                pool.nop(nofuse=True)
                for t in range(TPU):
                    last = nc.gpsimd.tensor_scalar(dst[:, s, t], src[:, t], nm[:, s, t:t + 1],
                                                   rst[:, s, t:t + 1], ALU.add, ALU.mult)
                last.then_inc(done, 1)

            def norm1(u):
                if not live(u):
                    return
                if begun(u, 2):
                    pool.wait_ge(hT_filled, count(u, 2))
                norm(u, xs[:, u.r], h, mv1, nm1, ve1, rs1, aggr1_done, nm1_done, rstd1_done, h_done)

            def norm2(u):
                if not live(u):
                    return
                if begun(u, 2):
                    pool.wait_ge(h2T_filled, count(u, 2))
                norm(u, x2[:, u.r % 2], h2, mv2, nm2, ve2, rs2, aggr2_done, nm2_done, rstd2_done, h2_done)

            def final_sum(u):
                if not live(u):
                    return
                s = u.r % 2
                pool.wait_ge(yc_done, count(u))
                if not isinstance(u.n, int) or u.n >= 2:
                    pool.wait_ge(out_done[s], (u.n - s) * 8)
                nc.gpsimd.tensor_tensor(ob[:, s], x2[:, s], yc[:, s], ALU.add).then_inc(ob_done, 1)

            def step(t):
                add_rope(unit(t, 1))
                gate(unit(t, 2))
                split_vsum(unit(t, 1))
                norm1(unit(t, 0))
                final_sum(unit(t, 3))
                norm2(unit(t, 2))

            run_steps(pool, step)

        @block.vector
        def _(dve):
            links = [0]

            def link(ins):
                links[0] += 1
                ins.then_inc(w_chain, 1)
                dve.wait_ge(w_chain, links[0])

            def setup():
                dve.wait_ge(c_in, 16 * N_LOADS)
                dve.wait_ge(setup_pe, 1)
                pw = p_num[:, 0:2, :].rearrange("p t d -> p (t d)").rearrange("p (w d) -> p w d", w=4)
                for n in range(2):
                    nc.vector.tensor_copy(w_qk[:, :, n].rearrange("p a (h f) -> p a h f", h=H),
                                          pw[:, n].rearrange("p (h a f) -> p a h f", h=H, a=2))
                nc.vector.tensor_copy(w_gv[:, 0], pw[:, 3])
                nc.vector.tensor_copy(w_gv[:, 1], pw[:, 2])
                link(nc.vector.tensor_copy(w_o[:], p_num[:, 2, 0:D]))
                link(nc.vector.reciprocal(rsc[:], sc[:]))
                nc.vector.tensor_tensor(ysc[:], sc[:, 0:1], sc[:, 1:2], ALU.mult)
                nc.vector.tensor_copy(identb[:], ident[:])
                nc.vector.tensor_copy(sel[:], sel_f[:])
                for r in range(2):
                    nc.vector.tensor_copy(vrow[:, r], vrow_f[:])
                link(nc.vector.tensor_tensor(qr[:, 0:1], rsc[:, 0:1], rsc[:, 0:1], ALU.mult))
                link(nc.vector.tensor_scalar(small[:, 0:1], qr[:, 0:1], SMALL ** 2, 1.0, ALU.is_le, ALU.mult))
                link(nc.vector.tensor_scalar(qv[:, 0:D], fw[:], rsc[:, 1:2], None, ALU.mult))
                round_e4m3fn(fwq[:], D, lambda n, ins: link(ins))

            def round_e4m3fn(dst, cols, link_nth):
                v, e, r, n = (b[:, 0:cols] for b in (qv, qe, qr, qn))
                link_nth(0, nc.vector.tensor_scalar(e.bitcast(I32), v.bitcast(I32), 0x7F800000, None,
                                                    ALU.bitwise_and))
                link_nth(1, nc.vector.tensor_scalar(e, e, 2.0 ** -6, 1.5 * 2.0 ** 20, ALU.max, ALU.mult))
                link_nth(2, nc.vector.tensor_tensor(r, v, e, ALU.add))
                link_nth(3, nc.vector.tensor_tensor(r, r, e, ALU.subtract))
                link_nth(4, nc.vector.tensor_tensor(n, r, r, ALU.mult))
                link_nth(5, nc.vector.tensor_scalar(n, n, 448.0 ** 2, 3e38, ALU.is_gt, ALU.mult))
                link_nth(6, nc.vector.tensor_scalar(n, n, 3e38, 0.0, ALU.mult, ALU.mult))
                link_nth(7, nc.vector.tensor_tensor(dst, r, n, ALU.add))

            def quantise_if_wide(u):
                if not live(u):
                    return
                def link_nth(n, ins):
                    ins.then_inc(rounding[n], 1)
                    dve.wait_ge(rounding[n], count(u))
                    dve.nop(nofuse=True)

                with dve.If(is_small == 0):
                    dve.wait_ge(h2T_filled, count(u))
                    if begun(u, 1):
                        dve.wait_ge(y_filled, count(u, 1))
                    dve.nop(nofuse=True)
                    link_nth(8, nc.vector.tensor_scalar(qv[:], p_h2T, rsc[:, 0:1], None, ALU.mult))
                    round_e4m3fn(q16[:], W, link_nth)
                    nc.vector.tensor_copy(qe[:, 0:1], rsc[:, 0:1]).then_inc(q8_done, 1)

            def rope(u):
                if not live(u):
                    return
                for j in range(BPU):
                    dve.wait_ge(qk_filled[j], count(u))
                    if begun(u, 1):
                        dve.wait_ge(qk_done[j], count(u, 1))
                    nc.vector.tensor_tensor(rc[:, j], p_qk[j][:], cos_t[:].rearrange("p a (h d) -> p a h d", h=2),
                                            ALU.mult)
                    nc.vector.tensor_tensor(rs[:, j], p_qk[j][:, :, ::-1, :],
                                            sin_t[:].rearrange("p a (h d) -> p a h d", h=2),
                                            ALU.mult).then_inc(rope_done[j], 1)

            def divide(u):
                if not live(u):
                    return
                dve.wait_ge(num_filled, count(u))
                nc.vector.reciprocal(rden[:], p_num[:, :, D:NW]).then_inc(rden_done, 1)
                dve.wait_ge(rden_done, count(u))
                nc.vector.tensor_tensor(t1[:].rearrange("p t (h e) -> p t h e", h=H),
                                        p_num[:, :, 0:D].rearrange("p t (h e) -> p t h e", h=H),
                                        rden[:].unsqueeze(3).to_broadcast([P, TPU, H, DK]),
                                        ALU.mult).then_inc(t1_done, 1)

            def add_lepe(u):
                if not live(u):
                    return
                dve.wait_ge(lepe_filled, count(u))
                dve.wait_ge(t1_done, count(u))
                if begun(u, 2):
                    dve.wait_ge(o_done, count(u, 2))
                nc.vector.tensor_tensor(t2[:, u.r % 2], t1[:], p_lepe[:], ALU.add).then_inc(t2_done, 1)

            def stats(u, src, st, mv, stats_done, aggr_done):
                for t in range(TPU):
                    last = nc.vector.bn_stats(st[:, u.r % 2, t], src[:, t])
                last.then_inc(stats_done, 1)
                dve.wait_ge(stats_done, count(u))
                dve.nop(nofuse=True)
                for t in range(TPU):
                    last = nc.vector.bn_aggr(mv[:, u.r % 2, t], st[:, u.r % 2, t])
                last.then_inc(aggr_done, 1)

            def stats1(u):
                if not live(u):
                    return
                dve.wait_ge(x_in[u.r], (u.n - u.r) * (16 // UNROLL) + 16)
                if begun(u, 2):
                    dve.wait_ge(h_done, count(u, 2))
                stats(u, xs[:, u.r], st1, mv1, stats1_done, aggr1_done)

            def conv(u):
                if not live(u):
                    return
                s = u.r % 2
                dve.wait_ge(vT_done, count(u))
                dve.wait_ge(tap0_done, count(u))
                for n, k in enumerate((0, 1, 3, 4)):
                    off = k - TAPS // 2
                    lo, hi = max(0, -off), min(S, S - off)
                    if n:
                        dve.wait_ge(conv_done[n - 1], count(u))
                    part = acc[:, s, :, lo:hi]
                    nc.vector.scalar_tensor_tensor(out=part, in0=vT[:, s, :, lo + off:hi + off],
                                                   scalar=conv_w[:, k:k + 1], in1=part, op0=ALU.mult,
                                                   op1=ALU.add).then_inc(conv_done[n], 1)

            def mask_kv(u):
                if not live(u):
                    return
                s = u.r % 2
                dve.wait_ge(kv_filled, count(u))
                if begun(u, 2):
                    dve.wait_ge(num_filled, count(u, 2))
                nc.vector.tensor_tensor(kvs[:, s, :, 0:D], p_kv[:, :, 0:D],
                                        mask[:].unsqueeze(1).to_broadcast([P, BPU, D]), ALU.mult)
                nc.vector.tensor_tensor(kvs[:, s, :, D:NW], p_kv[:, :, D:D + 1].to_broadcast([P, BPU, H]),
                                        hmask[:].unsqueeze(1).to_broadcast([P, BPU, H]),
                                        ALU.mult).then_inc(kvs_done, 1)

            def residual(u):
                if not live(u):
                    return
                s = u.r % 2
                dve.wait_ge(proj_filled, count(u))
                if begun(u, 2):
                    dve.wait_ge(ob_done, count(u, 2))
                nc.vector.tensor_tensor(x2[:, s], xs[:, u.r], p_proj, ALU.add).then_inc(x2_done, 1)
                dve.wait_ge(x2_done, count(u))
                stats(u, x2[:, s], st2, mv2, stats2_done, aggr2_done)

            def add_bias(u):
                if not live(u):
                    return
                s = u.r % 2
                dve.wait_ge(yb_done, count(u))
                nc.vector.tensor_tensor(yc[:, s], yb[:, s], fb[:].unsqueeze(1).to_broadcast([P, TPU, D]),
                                        ALU.add).then_inc(yc_done, 1)

            def step(t):
                rope(unit(t, 1))
                quantise_if_wide(unit(t, 3))
                divide(unit(t, 2))
                add_lepe(unit(t, 2))
                stats1(unit(t, 0))
                conv(unit(t, 1))
                mask_kv(unit(t, 1))
                add_bias(unit(t, 3))
                residual(unit(t, 2))

            setup()
            nc.vector.tensor_copy(qe[:, 0:1], ysc[:]).then_inc(w_ready, 1)
            dve.wait_ge(w_ready, 1)
            is_small = dve.value_load(small[0:1, 0:1], min_val=0, max_val=1)
            run_steps(dve, step)

        @block.tensor
        def _(pe):
            pe.wait_ge(c_in, 16 * N_LOADS)
            for n in range(4):
                nc.tensor.transpose(p_num[:, n // 2, (n % 2) * D:(n % 2 + 1) * D], w_raw[:, n], ident[:])
            nc.tensor.transpose(p_num[:, 2, 0:D], w_raw[:, 4], ident[:]).then_inc(setup_pe, 1)
            pe.wait_ge(w_ready, 1)
            pe.wait_ge(const_set, 2)
            is_small = pe.value_load(small[0:1, 0:1], min_val=0, max_val=1)

            def qk_tile(u, q_or_k, t):
                a = t % TPB
                return qk[:, u.r % 2, t // TPB, q_or_k, 2 * a:2 * a + 2].rearrange("p h d -> p (h d)")

            def attend(u):
                if not live(u):
                    return
                s = u.r % 2
                pe.wait_ge(qT_done, count(u))
                pe.wait_ge(kvs_done, count(u))
                pe.wait_ge(vrow_done, count(u))
                if begun(u, 1):
                    pe.wait_ge(x2_done, count(u, 1))
                for t in range(TPU):
                    j = t // TPB
                    nc.tensor.matmul(p_num[:, t, 0:NW], qT[:, s, t * P:(t + 1) * P], kvs[:, s, j],
                                     start=True, stop=False)
                    last = nc.tensor.matmul(p_num[:, t, 0:NW], sel[:, j], vrow[:, s], start=False, stop=True)
                last.then_inc(num_filled, 1)

            def transpose_lepe(u):
                if not live(u):
                    return
                s = u.r % 2
                pe.wait_ge(conv_done[-1], count(u))
                if begun(u, 1):
                    pe.wait_ge(t2_done, count(u, 1))
                for t in range(TPU):
                    a = t % TPB
                    last = nc.tensor.transpose(p_lepe[:, t], acc[:, s, t // TPB, a * P:(a + 1) * P], ident[:])
                last.then_inc(lepe_filled, 1)

            def transpose_h2(u):
                if not live(u):
                    return
                s = u.r % 2
                pe.wait_ge(h2_done, count(u))
                pe.wait_ge(hT_done, count(u, -2))
                for t in range(TPU):
                    last = nc.tensor.transpose(p_h2T[:, t * P:(t + 1) * P], h2[:, s, t], identb[:])
                last.then_inc(h2T_filled, 1)

            def transpose_v(u):
                if not live(u):
                    return
                pe.wait_ge(gv_done[0], count(u))
                pe.wait_ge(gv_done[1], count(u))
                for t in range(TPU):
                    a = t % TPB
                    last = nc.tensor.transpose(p_vT[:, t // TPB, a * P:(a + 1) * P], gv[:, u.r, t, D:2 * D], ident[:])
                last.then_inc(vT_filled, 1)

            def ffn(u):
                if not live(u):
                    return
                s = u.r % 2
                pe.wait_ge(q8_done, count(u))
                pe.wait_ge(gv_done[1], count(u, -2))
                pe.nop(nofuse=True)

                def products(q):
                    for t in range(TPU):
                        last = nc.tensor.matmul(p_y[:, t * P:(t + 1) * P], q[:, t * P:(t + 1) * P], fwq[:],
                                                start=True, stop=True)
                    last.then_inc(y_filled, 1)

                with pe.If(is_small == 1):
                    products(q8[:, s])
                with pe.If(is_small == 0):
                    products(q16)

            def transpose_q(u):
                if not live(u):
                    return
                pe.wait_ge(qk_done[0], count(u))
                pe.wait_ge(qk_done[1], count(u))
                if begun(u, 2):
                    pe.wait_ge(q8_done, count(u, 2))
                for t in range(TPU):
                    last = nc.tensor.transpose(p_t[:, t * P:(t + 1) * P], qk_tile(u, 0, t), ident[:])
                last.then_inc(qT_filled, 1)

            def key_value(u):
                if not live(u):
                    return
                if begun(u, 1):
                    pe.wait_ge(t1_done, count(u, 1))
                for t in range(TPU):
                    last = nc.tensor.matmul(p_kv[:, t // TPB, 0:D + 1], qk_tile(u, 1, t), gv[:, u.r, t, D:2 * D + 1],
                                            start=(t % TPB == 0), stop=(t % TPB == TPB - 1))
                last.then_inc(kv_filled, 1)

            def vsum_rows(u):
                if not live(u):
                    return
                s = u.r % 2
                pe.wait_ge(vsp_done, count(u))
                pe.wait_ge(tap0_done, count(u))
                nc.tensor.matmul(p_vrow, vsp[:, s].rearrange("p j c -> p (j c)"), identb[:], start=True,
                                 stop=True).then_inc(vrow_filled, 1)

            def transpose_o(u):
                if not live(u):
                    return
                s = u.r % 2
                pe.wait_ge(o_done, count(u))
                if begun(u, 1):
                    pe.wait_ge(yb_done, count(u, 1))
                for t in range(TPU):
                    last = nc.tensor.transpose(p_oT[:, t * P:(t + 1) * P], o[:, s, t], ident[:])
                last.then_inc(oT_filled, 1)

            def transpose_h(u):
                if not live(u):
                    return
                s = u.r % 2
                pe.wait_ge(h_done, count(u))
                if begun(u, 1):
                    pe.wait_ge(qT_done, count(u, 1))
                for t in range(TPU):
                    last = nc.tensor.transpose(p_t[:, t * P:(t + 1) * P], h[:, s, t], ident[:])
                last.then_inc(hT_filled, 1)

            def project_o(u):
                if not live(u):
                    return
                s = u.r % 2
                pe.wait_ge(oT_done, count(u))
                pe.wait_ge(t1_done, count(u))
                for t in range(TPU):
                    last = nc.tensor.matmul(p_proj[:, t], oT[:, s, t * P:(t + 1) * P], w_o[:], start=True, stop=True)
                last.then_inc(proj_filled, 1)

            def project_h(u):
                if not live(u):
                    return
                s = u.r % 2
                pe.wait_ge(hT_done, count(u))
                if begun(u, 1):
                    pe.wait_ge(vrow_done, count(u, 1))
                if begun(u, 2):
                    pe.wait_ge(oT_done, count(u, 2))
                for j in range(BPU):
                    if begun(u, 1):
                        pe.wait_ge(rope_done[j], count(u, 1))
                    for a in range(TPB):
                        t = TPB * j + a
                        lq = nc.tensor.matmul(p_qk[j][:, a].rearrange("p h d -> p (h d)"), hT[:, s, t * P:(t + 1) * P],
                                              w_qk[:].rearrange("p a q d -> p (a q d)"), start=True, stop=True)
                        lg = nc.tensor.matmul(p_gv[j][:, a], hT[:, s, t * P:(t + 1) * P],
                                              w_gv[:].rearrange("p g d -> p (g d)"), start=True, stop=True)
                        if a == TPB - 1:
                            lq.then_inc(qk_filled[j], 1)
                            lg.then_inc(gv_filled[j], 1)

            def step(t):
                attend(unit(t, 2))
                transpose_lepe(unit(t, 2))
                transpose_h2(unit(t, 3))
                transpose_v(unit(t, 1))
                ffn(unit(t, 3))
                transpose_q(unit(t, 1))
                key_value(unit(t, 1))
                vsum_rows(unit(t, 1))
                transpose_h(unit(t, 0))
                transpose_o(unit(t, 2))
                project_o(unit(t, 2))
                project_h(unit(t, 0))

            run_steps(pe, step)


N_LOADS = 18
N_ROUNDING = 9
SMALL = 21.0
_INS = ["L0_attn_hidden_states", "L0_attn_Wq", "L0_attn_Wk", "L0_attn_Wv", "L0_attn_Wg", "L0_attn_Wo",
        "L0_attn_lepe_w", "L0_attn_lepe_b", "L0_ffn_kernel", "L0_ffn_input_scale", "L0_ffn_kernel_scale",
        "L0_ffn_bias"]


def shape_constants():
    import numpy as np
    f32 = np.float32
    inv = (1.0 / np.float32(ROPE_BASE) ** (np.arange(0, DK, 2, dtype=f32) / np.float32(DK))).astype(f32)
    ang = np.arange(S, dtype=f32)[:, None] * inv[None, :]
    tab = ang.reshape(TPB, P, 1, HALF).transpose(1, 0, 2, 3)
    tab = np.broadcast_to(tab, (P, TPB, 2 * H, HALF)).reshape(P, TPB, D)
    cos, sin = np.cos(tab).astype(f32), np.sin(tab).astype(f32)
    cos_c = np.concatenate([cos, cos], axis=-1)
    sin_c = np.concatenate([-sin, sin], axis=-1)
    row_head = (np.arange(D) % (D // 2)) // HALF
    col_head = np.arange(D) // DK
    scale = f32(DK) ** f32(-0.5)
    mask = (row_head[:, None] == col_head[None, :]).astype(f32) * scale
    hmask = (row_head[:, None] == np.arange(H)[None, :]).astype(f32) * scale
    sel = np.repeat((np.arange(3 * BPU)[:, None] // 3 == np.arange(BPU)[None, :])[:, :, None], P, 2)
    vrow = np.zeros((3 * BPU, NW), f32)
    vrow[::3, D:] = S
    return {"cos": cos_c, "sin": sin_c, "ident": np.eye(P, dtype=f32),
            "mask": mask, "hmask": hmask, "sel": sel.astype(f32), "vrow": vrow}


def kernel(**inputs):
    import numpy as _np
    import concourse.bacc as _bacc
    from concourse import mybir as _mybir
    from concourse.bass_utils import run_bass_kernel_spmd as _run

    nc = _bacc.Bacc("TRN2", target_bir_lowering=False, num_devices=1)
    arrays, args = {}, []
    named = [(n, _np.ascontiguousarray(inputs[n])) for n in _INS] + list(shape_constants().items())
    for name, a in named:
        arrays[f"in_{name}_dram"] = a
        args.append(nc.dram_tensor(f"in_{name}_dram", a.shape, _mybir.dt.from_np(a.dtype), kind="ExternalInput").ap())
    args.append(nc.dram_tensor("out_dram", (B, S, D), F32, kind="ExternalOutput").ap())
    build(nc, *args)
    r = _run(nc, [arrays], core_ids=[0])
    return r.results[0]["out_dram"]
```

```python
from collections import namedtuple
from contextlib import ExitStack

import concourse.bass as bass
from concourse import mybir

P = 128
D = 128
B, S = 32, 256
H, DK = 8, 16
HALF = DK // 2
TAPS = 5
EPS = 1e-5
ROPE_BASE = 10000.0

TPB = S // P
BPU = 2
TPU = TPB * BPU
U = B // BPU
W = TPU * P
DEN = H
NW = D + DEN
LAG = 3
UNROLL = 4

F32 = mybir.dt.float32
BF16 = mybir.dt.bfloat16
F8 = mybir.dt.float8e4
I32 = mybir.dt.int32
ALU = mybir.AluOpType
ACT = mybir.ActivationFunctionType

Unit = namedtuple("Unit", "n r")


def unit(step, back):
    return Unit(step.n - back, (step.r - back) % UNROLL)


def live(u):
    return not isinstance(u.n, int) or 0 <= u.n < U


def begun(u, back):
    return not isinstance(u.n, int) or u.n >= back


def count(u, back=0):
    n = u.n - back
    return min(n, U - 1) + 1 if isinstance(n, int) else n + 1


def run_steps(eng, step):
    for t in range(UNROLL):
        step(Unit(t, t % UNROLL))
    with eng.Fori(UNROLL, U, UNROLL) as i:
        for k in range(UNROLL):
            step(Unit(i + k, k))
    for t in range(U, U + LAG):
        step(Unit(t, t % UNROLL))


def build(nc, x, wq, wk, wv, wg, wo, lepe_w, lepe_b, ffn_w, s_in, s_k, ffn_b,
          cos_c, sin_c, ident_c, mask_c, hmask_c, sel_c, vrow_c, out):
    ctx = ExitStack()
    with ctx:
        def sb(name, shape, dt=F32):
            return ctx.enter_context(nc.sbuf_tensor(name, shape, dt))

        def ps(name, shape):
            return ctx.enter_context(nc.psum_tensor(name, shape, F32))

        def sem(name):
            return ctx.enter_context(nc.semaphore(name))

        cos_t = sb("cos_t", [P, TPB, 2 * D])
        sin_t = sb("sin_t", [P, TPB, 2 * D])
        ident = sb("ident", [P, P])
        identb = sb("identb", [P, P], BF16)
        mask = sb("mask", [P, D])
        hmask = sb("hmask", [P, H])
        sel = sb("sel", [3 * BPU, BPU, P], BF16)
        sel_f = sb("sel_f", [3 * BPU, BPU, P])
        vrow_f = sb("vrow_f", [3 * BPU, NW])
        w_raw = sb("w_raw", [P, 5, D])
        w_qk = sb("w_qk", [P, 2, 2, D // 2])
        w_gv = sb("w_gv", [P, 2, D])
        w_o = sb("w_o", [P, D])
        conv_w = sb("conv_w", [P, TAPS])
        conv_b = sb("conv_b", [P, 1])
        fw = sb("fw", [P, D], BF16)
        fwq = sb("fwq", [P, D], BF16)
        fb = sb("fb", [P, D], BF16)
        sc = sb("sc", [P, 2])
        rsc = sb("rsc", [P, 2])
        ysc = sb("ysc", [P, 1])
        small = sb("small", [P, 2], I32)
        qv = sb("qv", [P, W])
        qe = sb("qe", [P, W])
        qr = sb("qr", [P, W])
        qn = sb("qn", [P, W])
        minus_half = sb("minus_half", [P, TPU])
        minus_one = sb("minus_one", [P, TPU])
        eps = sb("eps", [P, TPU])

        xs = sb("xs", [P, UNROLL, TPU, D])
        st1 = sb("st1", [P, 2, TPU, 6])
        mv1 = sb("mv1", [P, 2, TPU, 2])
        nm1 = sb("nm1", [P, 2, TPU])
        ve1 = sb("ve1", [P, 2, TPU])
        rs1 = sb("rs1", [P, 2, TPU])
        nmr1 = sb("nmr1", [P, 2, TPU])
        h = sb("h", [P, 2, TPU, D])
        hT = sb("hT", [P, 2, W])
        rc = sb("rc", [P, BPU, TPB, 2, D])
        rs = sb("rs", [P, BPU, TPB, 2, D])
        qk = sb("qk", [P, 2, BPU, 2, TPB * 2, D // 2])
        gv = sb("gv", [P, UNROLL, TPU, 2 * D + 1])
        qT = sb("qT", [P, 2, W])
        vT = sb("vT", [P, 2, BPU, S])
        vsum = sb("vsum", [P, 2, BPU])
        vres = sb("vres", [P, 2, BPU])
        vsp = sb("vsp", [P, 2, BPU, 3], BF16)
        vrow = sb("vrow", [3 * BPU, 2, NW], BF16)
        kvs = sb("kvs", [P, 2, BPU, NW])
        acc = sb("acc", [P, 2, BPU, S])
        rden = sb("rden", [P, TPU, H])
        t1 = sb("t1", [P, TPU, D])
        t2 = sb("t2", [P, 2, TPU, D])
        o = sb("o", [P, 2, TPU, D])
        oT = sb("oT", [P, 2, W])
        x2 = sb("x2", [P, 2, TPU, D])
        st2 = sb("st2", [P, 2, TPU, 6])
        mv2 = sb("mv2", [P, 2, TPU, 2])
        nm2 = sb("nm2", [P, 2, TPU])
        ve2 = sb("ve2", [P, 2, TPU])
        rs2 = sb("rs2", [P, 2, TPU])
        nmr2 = sb("nmr2", [P, 2, TPU])
        h2 = sb("h2", [P, 2, TPU, D], BF16)
        q8 = sb("q8", [P, 2, W], F8)
        q16 = sb("q16", [P, W], BF16)
        yb = sb("yb", [P, 2, TPU, D], BF16)
        yc = sb("yc", [P, 2, TPU, D], BF16)
        ob = sb("ob", [P, 2, TPU, D])

        p_qk = [ps(f"p_qk{j}", [P, TPB, 2, D]) for j in range(BPU)]
        p_gv = [ps(f"p_gv{j}", [P, TPB, 2 * D]) for j in range(BPU)]
        p_num = ps("p_num", [P, TPU, 2 * D])
        p_lepe = ps("p_lepe", [P, TPU, D])
        p_t = ps("p_t", [P, W])
        p_vT = p_gv[0][:, :, :].rearrange("p a d -> p (a d)").rearrange("p (j s) -> p j s", j=BPU)
        p_vrow = p_qk[0][0:3 * BPU, 0, 0, :]
        p_hT = p_gv[1][:, :, :].rearrange("p a d -> p (a d)")
        p_oT = p_lepe[:, :, :].rearrange("p t d -> p (t d)")
        p_qT, p_y = p_t, p_t
        p_kv = p_num[:, 0:2, :]
        p_proj = p_num[:, 2:4, :].rearrange("p t d -> p (t d)").rearrange("p (t d) -> p t d", t=TPU)
        p_h2T = p_t[:, 0:W // 2].bitcast(BF16)

        x_in = [sem(f"x_in{r}") for r in range(UNROLL)]
        c_in = sem("c_in")
        ob_free = [sem(f"ob_free{r}") for r in range(2)]
        setup_pe = sem("setup_pe")
        setup_dve = sem("setup_dve")
        w_ready = sem("w_ready")
        rounding = [sem(f"rounding{n}") for n in range(N_ROUNDING)]
        w_chain = sem("w_chain")
        const_set = sem("const_set")
        stats1_done = sem("stats1_done")
        aggr1_done = sem("aggr1_done")
        nm1_done = sem("nm1_done")
        pow1_done = sem("pow1_done")
        rstd1_done = sem("rstd1_done")
        h_done = sem("h_done")
        hT_filled = sem("hT_filled")
        hT_done = sem("hT_done")
        qk_filled = [sem(f"qk_filled{j}") for j in range(BPU)]
        gv_filled = [sem(f"gv_filled{j}") for j in range(BPU)]
        gv_done = [sem(f"gv_done{j}") for j in range(BPU)]
        rope_done = [sem(f"rope_done{j}") for j in range(BPU)]
        qk_done = [sem(f"qk_done{j}") for j in range(BPU)]
        vT_filled = sem("vT_filled")
        vT_done = sem("vT_done")
        tap0_done = sem("tap0_done")
        conv_done = [sem(f"conv_done{j}") for j in range(TAPS - 1)]
        vsp1 = sem("vsp1")
        vsp2 = sem("vsp2")
        vsp_done = sem("vsp_done")
        vrow_filled = sem("vrow_filled")
        vrow_done = sem("vrow_done")
        qT_filled = sem("qT_filled")
        qT_done = sem("qT_done")
        kv_filled = sem("kv_filled")
        kvs_done = sem("kvs_done")
        num_filled = sem("num_filled")
        rden_done = sem("rden_done")
        t1_done = sem("t1_done")
        lepe_filled = sem("lepe_filled")
        t2_done = sem("t2_done")
        o_done = sem("o_done")
        oT_filled = sem("oT_filled")
        oT_done = sem("oT_done")
        proj_filled = sem("proj_filled")
        x2_done = sem("x2_done")
        stats2_done = sem("stats2_done")
        aggr2_done = sem("aggr2_done")
        nm2_done = sem("nm2_done")
        pow2_done = sem("pow2_done")
        rstd2_done = sem("rstd2_done")
        h2_done = sem("h2_done")
        h2T_filled = sem("h2T_filled")
        q8_done = sem("q8_done")
        y_filled = sem("y_filled")
        yb_done = sem("yb_done")
        yc_done = sem("yc_done")
        ob_done = sem("ob_done")

        x_v = x.rearrange("(u j) (a p) d -> u p (j a) d", j=BPU, p=P)
        out_v = out.rearrange("(u j) (a p) d -> u p (j a) d", j=BPU, p=P)
        block = ctx.enter_context(nc.Block())

        @block.sync
        def _(sp):
            def load_x(u):
                if begun(u, UNROLL):
                    sp.wait_ge(x2_done, count(u, UNROLL))
                sp.dma_start(xs[:, u.r], x_v[u.n]).then_inc(x_in[u.r], 16)

            def store(u):
                if not live(u):
                    return
                sp.wait_ge(ob_done, count(u))
                sp.dma_start(out_v[u.n], ob[:, u.r % 2]).then_inc(ob_free[u.r % 2], 16)

            load_x(Unit(0, 0))

            def step(t):
                if live(unit(t, 3)):
                    store(unit(t, 3))
                if live(unit(t, -1)):
                    load_x(unit(t, -1))

            for t in range(UNROLL):
                step(Unit(t, t))
            with sp.Fori(UNROLL, U - UNROLL, UNROLL) as i:
                for k in range(UNROLL):
                    step(Unit(i + k, k))
            for t in range(U - UNROLL, U + LAG):
                step(Unit(t, t % UNROLL))
            for r in range(2):
                sp.wait_ge(ob_free[r], 16 + 16 * (U // 2))

        @block.scalar
        def _(act):
            loads = [(w_raw[:, n], w) for n, w in enumerate((wq, wk, wv, wg, wo))]
            loads += [(ident[:], ident_c), (cos_t[:], cos_c), (sin_t[:], sin_c),
                      (mask[:], mask_c), (hmask[:], hmask_c), (sel_f[:], sel_c), (vrow_f[:], vrow_c),
                      (conv_w[:], lepe_w.rearrange("c a k -> c (a k)")),
                      (conv_b[:], lepe_b.rearrange("(c a) -> c a", a=1)), (fw[:], ffn_w),
                      (fb[:], ffn_b.rearrange("(a c) -> a c", a=1).broadcast_to([P, D])),
                      (sc[:, 0:1], s_in.rearrange("(a c) -> a c", a=1).broadcast_to([P, 1])),
                      (sc[:, 1:2], s_k.rearrange("(a c) -> a c", a=1).broadcast_to([P, 1]))]
            for dst, src in loads:
                act.dma_start(dst, src).then_inc(c_in, 16)
            assert len(loads) == N_LOADS
            act.wait_ge(c_in, 16 * N_LOADS)

            def quantise(u):
                act.wait_ge(h2T_filled, count(u))
                if begun(u, 1):
                    act.wait_ge(y_filled, count(u, 1))
                act.nop(nofuse=True)
                nc.scalar.activation(q8[:, u.r % 2], p_h2T, ACT.Copy, scale=rsc[:, 0:1],
                                     saturate=False).then_inc(q8_done, 1)

            def norm1(u):
                if not live(u):
                    return
                s = u.r % 2
                act.wait_ge(rstd1_done, count(u))
                if begun(u, 2):
                    act.wait_ge(hT_filled, count(u, 2))
                for t in range(TPU):
                    last = nc.scalar.activation(h[:, s, t], xs[:, u.r, t], ACT.Identity, scale=rs1[:, s, t:t + 1],
                                                bias=nmr1[:, s, t:t + 1])
                last.then_inc(h_done, 1)

            def norm2(u):
                if not live(u):
                    return
                s = u.r % 2
                act.wait_ge(rstd2_done, count(u))
                if begun(u, 1):
                    act.wait_ge(h2T_filled, count(u, 1))
                for t in range(TPU):
                    last = nc.scalar.activation(h2[:, s, t], x2[:, s, t], ACT.Identity, scale=rs2[:, s, t:t + 1],
                                                bias=nmr2[:, s, t:t + 1])
                last.then_inc(h2_done, 1)

            def quantise_if_small(u):
                if not live(u):
                    return
                with act.If(is_small == 1):
                    quantise(u)

            def move_vT(u):
                if not live(u):
                    return
                act.wait_ge(vT_filled, count(u))
                if begun(u, 2):
                    act.wait_ge(vsp_done, count(u, 2))
                if begun(u, 2):
                    act.wait_ge(conv_done[-1], count(u, 2))
                for j in range(BPU):
                    last = nc.scalar.activation(vT[:, u.r % 2, j], p_vT[:, j], ACT.Copy,
                                                accum_out=vsum[:, u.r % 2, j:j + 1])
                last.then_inc(vT_done, 1)
                if begun(u, 2):
                    act.wait_ge(lepe_filled, count(u, 2))
                nc.scalar.activation(acc[:, u.r % 2], p_vT, ACT.Identity, scale=conv_w[:, TAPS // 2:TAPS // 2 + 1],
                                     bias=conv_b[:, 0:1]).then_inc(tap0_done, 1)

            def move_y(u):
                if not live(u):
                    return
                act.wait_ge(y_filled, count(u))
                if begun(u, 1):
                    act.wait_ge(yc_done, count(u, 1))
                nc.scalar.activation(yb[:, u.r % 2], p_y[:].rearrange("p (t d) -> p t d", t=TPU), ACT.Copy,
                                     scale=ysc[:, 0:1]).then_inc(yb_done, 1)

            def move_qT(u):
                if not live(u):
                    return
                act.wait_ge(qT_filled, count(u))
                if begun(u, 2):
                    act.wait_ge(num_filled, count(u, 2))
                nc.scalar.activation(qT[:, u.r % 2], p_qT[:], ACT.Copy).then_inc(qT_done, 1)

            def move_vrow(u):
                if not live(u):
                    return
                act.wait_ge(vrow_filled, count(u))
                nc.scalar.activation(vrow[:, u.r % 2, 0:D], p_vrow, ACT.Copy).then_inc(vrow_done, 1)

            def move_oT(u):
                if not live(u):
                    return
                act.wait_ge(oT_filled, count(u))
                if begun(u, 2):
                    act.wait_ge(proj_filled, count(u, 2))
                nc.scalar.activation(oT[:, u.r % 2], p_oT, ACT.Copy).then_inc(oT_done, 1)

            def move_hT(u):
                if not live(u):
                    return
                act.wait_ge(hT_filled, count(u))
                if begun(u, 2):
                    act.wait_ge(gv_filled[-1], count(u, 2))
                nc.scalar.activation(hT[:, u.r % 2], p_hT, ACT.Copy).then_inc(hT_done, 1)

            def move_gv(u, j):
                if not live(u):
                    return
                act.wait_ge(gv_filled[j], count(u))
                if begun(u, 3):
                    act.wait_ge(o_done, count(u, 3))
                nc.scalar.activation(gv[:, u.r, TPB * j:TPB * (j + 1), 0:2 * D], p_gv[j][:],
                                     ACT.Copy).then_inc(gv_done[j], 1)

            def step(t):
                move_gv(unit(t, 1), 0)
                move_oT(unit(t, 2))
                move_gv(unit(t, 1), 1)
                move_vT(unit(t, 1))
                move_qT(unit(t, 1))
                move_vrow(unit(t, 1))
                norm2(unit(t, 2))
                norm1(unit(t, 0))
                quantise_if_small(unit(t, 2))
                move_hT(unit(t, 0))
                move_y(unit(t, 2))

            act.wait_ge(w_ready, 1)
            is_small = act.value_load(small[0:1, 0:1], min_val=0, max_val=1)
            run_steps(act, step)

        @block.gpsimd
        def _(pool):
            nc.gpsimd.memset(minus_half[:], -0.5)
            nc.gpsimd.memset(minus_one[:], -1.0)
            nc.gpsimd.memset(eps[:], EPS)
            for r in range(2):
                nc.gpsimd.memset(ob[:, r, 0, 0:1], 0.0).then_inc(ob_free[r], 16)
            nc.gpsimd.memset(gv[:, :, :, 2 * D:2 * D + 1], 1.0).then_inc(const_set, 1)
            pool.wait_ge(const_set, 1)

            def add_rope(u):
                if not live(u):
                    return
                for j in range(BPU):
                    pool.wait_ge(rope_done[j], count(u))
                    if begun(u, 2):
                        pool.wait_ge(kv_filled, count(u, 2))
                    nc.gpsimd.tensor_tensor(
                        qk[:, u.r % 2, j].rearrange("p q t d -> p t q d"),
                        rc[:, j].rearrange("p a h (q d) -> p (a h) q d", q=2),
                        rs[:, j].rearrange("p a h (q d) -> p (a h) q d", q=2), ALU.add).then_inc(qk_done[j], 1)

            def gate(u):
                if not live(u):
                    return
                pool.wait_ge(t2_done, count(u))
                if begun(u, 2):
                    pool.wait_ge(oT_filled, count(u, 2))
                nc.gpsimd.tensor_tensor(o[:, u.r % 2], t2[:, u.r % 2], gv[:, u.r, :, 0:D],
                                        ALU.mult).then_inc(o_done, 1)

            def split_vsum(u):
                if not live(u):
                    return
                s = u.r % 2
                pool.wait_ge(vT_done, count(u))
                if begun(u, 2):
                    pool.wait_ge(vrow_filled, count(u, 2))
                pool.nop(nofuse=True)
                nc.gpsimd.tensor_scalar(vsp[:, s, :, 0], vsum[:, s], 1.0, 0.0, ALU.mult,
                                        ALU.add).then_inc(vsp1, 1)
                pool.wait_ge(vsp1, count(u))
                nc.gpsimd.tensor_tensor(vres[:, s], vsum[:, s], vsp[:, s, :, 0], ALU.subtract)
                nc.gpsimd.tensor_tensor(vsp[:, s, :, 1], vsum[:, s], vsp[:, s, :, 0],
                                        ALU.subtract).then_inc(vsp2, 1)
                pool.wait_ge(vsp2, count(u))
                nc.gpsimd.tensor_tensor(vsp[:, s, :, 2], vres[:, s], vsp[:, s, :, 1],
                                        ALU.subtract).then_inc(vsp_done, 1)

            def rstd(u, mv, nm, ve, rst, nmr, aggr_done, nm_done, pow_done, rstd_done):
                s = u.r % 2
                pool.wait_ge(aggr_done, count(u))
                nc.gpsimd.tensor_tensor(nm[:, s], mv[:, s, :, 0], minus_one[:], ALU.mult)
                nc.gpsimd.tensor_tensor(ve[:, s], mv[:, s, :, 1], eps[:], ALU.add).then_inc(nm_done, 1)
                pool.wait_ge(nm_done, count(u))
                nc.gpsimd.tensor_tensor(rst[:, s], ve[:, s], minus_half[:], ALU.pow).then_inc(pow_done, 1)
                pool.wait_ge(pow_done, count(u))
                nc.gpsimd.tensor_tensor(nmr[:, s], nm[:, s], rst[:, s], ALU.mult).then_inc(rstd_done, 1)

            def rstd1(u):
                if not live(u):
                    return
                if begun(u, 2):
                    pool.wait_ge(h_done, count(u, 2))
                rstd(u, mv1, nm1, ve1, rs1, nmr1, aggr1_done, nm1_done, pow1_done, rstd1_done)

            def rstd2(u):
                if not live(u):
                    return
                if begun(u, 1):
                    pool.wait_ge(h2_done, count(u, 1))
                rstd(u, mv2, nm2, ve2, rs2, nmr2, aggr2_done, nm2_done, pow2_done, rstd2_done)

            def final_sum(u):
                if not live(u):
                    return
                s = u.r % 2
                pool.wait_ge(yc_done, count(u))
                pool.wait_ge(ob_free[s], (u.n - s) * 8 + 16)
                nc.gpsimd.tensor_tensor(ob[:, s], x2[:, s], yc[:, s], ALU.add).then_inc(ob_done, 1)

            def step(t):
                gate(unit(t, 2))
                add_rope(unit(t, 1))
                split_vsum(unit(t, 1))
                rstd2(unit(t, 2))
                rstd1(unit(t, 0))
                final_sum(unit(t, 3))

            run_steps(pool, step)

        @block.vector
        def _(dve):
            links = [0]

            def link(ins):
                links[0] += 1
                ins.then_inc(w_chain, 1)
                dve.wait_ge(w_chain, links[0])

            def setup():
                dve.wait_ge(c_in, 16 * N_LOADS)
                dve.wait_ge(setup_pe, 1)
                pw = p_num[:, 0:2, :].rearrange("p t d -> p (t d)").rearrange("p (w d) -> p w d", w=4)
                for n in range(2):
                    nc.vector.tensor_copy(w_qk[:, :, n].rearrange("p a (h f) -> p a h f", h=H),
                                          pw[:, n].rearrange("p (h a f) -> p a h f", h=H, a=2))
                nc.vector.tensor_copy(w_gv[:, 0], pw[:, 3])
                nc.vector.tensor_copy(w_gv[:, 1], pw[:, 2])
                link(nc.vector.tensor_copy(w_o[:], p_num[:, 2, 0:D]))
                link(nc.vector.reciprocal(rsc[:], sc[:]))
                nc.vector.tensor_tensor(ysc[:], sc[:, 0:1], sc[:, 1:2], ALU.mult)
                nc.vector.tensor_copy(identb[:], ident[:])
                nc.vector.tensor_copy(sel[:], sel_f[:])
                for r in range(2):
                    nc.vector.tensor_copy(vrow[:, r], vrow_f[:])
                link(nc.vector.tensor_tensor(qr[:, 0:1], rsc[:, 0:1], rsc[:, 0:1], ALU.mult))
                link(nc.vector.tensor_scalar(small[:, 0:1], qr[:, 0:1], SMALL ** 2, 1.0, ALU.is_le, ALU.mult))
                link(nc.vector.tensor_scalar(qv[:, 0:D], fw[:], rsc[:, 1:2], None, ALU.mult))
                round_e4m3fn(fwq[:], D, lambda n, ins: link(ins))

            def round_e4m3fn(dst, cols, link_nth):
                v, e, r, n = (b[:, 0:cols] for b in (qv, qe, qr, qn))
                link_nth(0, nc.vector.tensor_scalar(e.bitcast(I32), v.bitcast(I32), 0x7F800000, None,
                                                    ALU.bitwise_and))
                link_nth(1, nc.vector.tensor_scalar(e, e, 2.0 ** -6, 1.5 * 2.0 ** 20, ALU.max, ALU.mult))
                link_nth(2, nc.vector.tensor_tensor(r, v, e, ALU.add))
                link_nth(3, nc.vector.tensor_tensor(r, r, e, ALU.subtract))
                link_nth(4, nc.vector.tensor_tensor(n, r, r, ALU.mult))
                link_nth(5, nc.vector.tensor_scalar(n, n, 448.0 ** 2, 3e38, ALU.is_gt, ALU.mult))
                link_nth(6, nc.vector.tensor_scalar(n, n, 3e38, 0.0, ALU.mult, ALU.mult))
                link_nth(7, nc.vector.tensor_tensor(dst, r, n, ALU.add))

            def quantise_if_wide(u):
                if not live(u):
                    return
                def link_nth(n, ins):
                    ins.then_inc(rounding[n], 1)
                    dve.wait_ge(rounding[n], count(u))
                    dve.nop(nofuse=True)

                with dve.If(is_small == 0):
                    dve.wait_ge(h2T_filled, count(u))
                    if begun(u, 1):
                        dve.wait_ge(y_filled, count(u, 1))
                    dve.nop(nofuse=True)
                    link_nth(8, nc.vector.tensor_scalar(qv[:], p_h2T, rsc[:, 0:1], None, ALU.mult))
                    round_e4m3fn(q16[:], W, link_nth)
                    nc.vector.tensor_copy(qe[:, 0:1], rsc[:, 0:1]).then_inc(q8_done, 1)

            def rope(u, j):
                if not live(u):
                    return
                dve.wait_ge(qk_filled[j], count(u))
                if begun(u, 1):
                    dve.wait_ge(qk_done[j], count(u, 1))
                nc.vector.tensor_tensor(rc[:, j], p_qk[j][:], cos_t[:].rearrange("p a (h d) -> p a h d", h=2),
                                        ALU.mult)
                nc.vector.tensor_tensor(rs[:, j], p_qk[j][:, :, ::-1, :],
                                        sin_t[:].rearrange("p a (h d) -> p a h d", h=2),
                                        ALU.mult).then_inc(rope_done[j], 1)

            def divide(u):
                if not live(u):
                    return
                dve.wait_ge(num_filled, count(u))
                nc.vector.reciprocal(rden[:], p_num[:, :, D:NW]).then_inc(rden_done, 1)
                dve.wait_ge(rden_done, count(u))
                nc.vector.tensor_tensor(t1[:].rearrange("p t (h e) -> p t h e", h=H),
                                        p_num[:, :, 0:D].rearrange("p t (h e) -> p t h e", h=H),
                                        rden[:].unsqueeze(3).to_broadcast([P, TPU, H, DK]),
                                        ALU.mult).then_inc(t1_done, 1)

            def add_lepe(u):
                if not live(u):
                    return
                dve.wait_ge(lepe_filled, count(u))
                dve.wait_ge(t1_done, count(u))
                if begun(u, 2):
                    dve.wait_ge(o_done, count(u, 2))
                nc.vector.tensor_tensor(t2[:, u.r % 2], t1[:], p_lepe[:], ALU.add).then_inc(t2_done, 1)

            def stats(u, src, st, mv, stats_done, aggr_done):
                for t in range(TPU):
                    last = nc.vector.bn_stats(st[:, u.r % 2, t], src[:, t])
                last.then_inc(stats_done, 1)
                dve.wait_ge(stats_done, count(u))
                dve.nop(nofuse=True)
                for t in range(TPU):
                    last = nc.vector.bn_aggr(mv[:, u.r % 2, t], st[:, u.r % 2, t])
                last.then_inc(aggr_done, 1)

            def stats1(u):
                if not live(u):
                    return
                dve.wait_ge(x_in[u.r], (u.n - u.r) * (16 // UNROLL) + 16)
                if begun(u, 2):
                    dve.wait_ge(h_done, count(u, 2))
                stats(u, xs[:, u.r], st1, mv1, stats1_done, aggr1_done)

            def conv(u, first, end):
                if not live(u):
                    return
                s = u.r % 2
                if first == 0:
                    dve.wait_ge(vT_done, count(u))
                    dve.wait_ge(tap0_done, count(u))
                for n in range(first, end):
                    k = (0, 1, 3, 4)[n]
                    off = k - TAPS // 2
                    lo, hi = max(0, -off), min(S, S - off)
                    if n:
                        dve.wait_ge(conv_done[n - 1], count(u))
                    part = acc[:, s, :, lo:hi]
                    nc.vector.scalar_tensor_tensor(out=part, in0=vT[:, s, :, lo + off:hi + off],
                                                   scalar=conv_w[:, k:k + 1], in1=part, op0=ALU.mult,
                                                   op1=ALU.add).then_inc(conv_done[n], 1)

            def mask_kv(u):
                if not live(u):
                    return
                s = u.r % 2
                dve.wait_ge(kv_filled, count(u))
                if begun(u, 2):
                    dve.wait_ge(num_filled, count(u, 2))
                nc.vector.tensor_tensor(kvs[:, s, :, 0:D], p_kv[:, :, 0:D],
                                        mask[:].unsqueeze(1).to_broadcast([P, BPU, D]), ALU.mult)
                nc.vector.tensor_tensor(kvs[:, s, :, D:NW], p_kv[:, :, D:D + 1].to_broadcast([P, BPU, H]),
                                        hmask[:].unsqueeze(1).to_broadcast([P, BPU, H]),
                                        ALU.mult).then_inc(kvs_done, 1)

            def residual(u):
                if not live(u):
                    return
                s = u.r % 2
                dve.wait_ge(proj_filled, count(u))
                if begun(u, 2):
                    dve.wait_ge(ob_done, count(u, 2))
                nc.vector.tensor_tensor(x2[:, s], xs[:, u.r], p_proj, ALU.add).then_inc(x2_done, 1)
                dve.wait_ge(x2_done, count(u))
                stats(u, x2[:, s], st2, mv2, stats2_done, aggr2_done)

            def add_bias(u):
                if not live(u):
                    return
                s = u.r % 2
                dve.wait_ge(yb_done, count(u))
                nc.vector.tensor_tensor(yc[:, s], yb[:, s], fb[:].unsqueeze(1).to_broadcast([P, TPU, D]),
                                        ALU.add).then_inc(yc_done, 1)

            def step(t):
                rope(unit(t, 1), 0)
                add_bias(unit(t, 3))
                rope(unit(t, 1), 1)
                residual(unit(t, 2))
                stats1(unit(t, 0))
                conv(unit(t, 1), 0, 2)
                mask_kv(unit(t, 1))
                conv(unit(t, 1), 2, 4)
                divide(unit(t, 1))
                quantise_if_wide(unit(t, 2))
                add_lepe(unit(t, 1))

            setup()
            nc.vector.tensor_copy(qe[:, 0:1], ysc[:]).then_inc(w_ready, 1)
            dve.wait_ge(w_ready, 1)
            is_small = dve.value_load(small[0:1, 0:1], min_val=0, max_val=1)
            run_steps(dve, step)

        @block.tensor
        def _(pe):
            pe.wait_ge(c_in, 16 * N_LOADS)
            for n in range(4):
                nc.tensor.transpose(p_num[:, n // 2, (n % 2) * D:(n % 2 + 1) * D], w_raw[:, n], ident[:])
            nc.tensor.transpose(p_num[:, 2, 0:D], w_raw[:, 4], ident[:]).then_inc(setup_pe, 1)
            pe.wait_ge(w_ready, 1)
            pe.wait_ge(const_set, 1)
            is_small = pe.value_load(small[0:1, 0:1], min_val=0, max_val=1)

            def qk_tile(u, q_or_k, t):
                a = t % TPB
                return qk[:, u.r % 2, t // TPB, q_or_k, 2 * a:2 * a + 2].rearrange("p h d -> p (h d)")

            def attend(u):
                if not live(u):
                    return
                s = u.r % 2
                pe.wait_ge(qT_done, count(u))
                pe.wait_ge(kvs_done, count(u))
                pe.wait_ge(vrow_done, count(u))
                if begun(u, 1):
                    pe.wait_ge(x2_done, count(u, 1))
                for t in range(TPU):
                    j = t // TPB
                    nc.tensor.matmul(p_num[:, t, 0:NW], qT[:, s, t * P:(t + 1) * P], kvs[:, s, j],
                                     start=True, stop=False)
                    last = nc.tensor.matmul(p_num[:, t, 0:NW], sel[:, j], vrow[:, s], start=False, stop=True)
                last.then_inc(num_filled, 1)

            def transpose_lepe(u):
                if not live(u):
                    return
                s = u.r % 2
                pe.wait_ge(conv_done[-1], count(u))
                if begun(u, 1):
                    pe.wait_ge(oT_done, count(u, 1))
                for t in range(TPU):
                    a = t % TPB
                    last = nc.tensor.transpose(p_lepe[:, t], acc[:, s, t // TPB, a * P:(a + 1) * P], ident[:])
                last.then_inc(lepe_filled, 1)

            def transpose_v(u):
                if not live(u):
                    return
                pe.wait_ge(gv_done[0], count(u))
                pe.wait_ge(gv_done[1], count(u))
                for t in range(TPU):
                    a = t % TPB
                    last = nc.tensor.transpose(p_vT[:, t // TPB, a * P:(a + 1) * P], gv[:, u.r, t, D:2 * D], ident[:])
                last.then_inc(vT_filled, 1)

            def transpose_h(u):
                if not live(u):
                    return
                s = u.r % 2
                pe.wait_ge(h_done, count(u))
                if begun(u, 1):
                    pe.wait_ge(gv_done[1], count(u, 1))
                for t in range(TPU):
                    last = nc.tensor.transpose(p_hT[:, t * P:(t + 1) * P], h[:, s, t], ident[:])
                last.then_inc(hT_filled, 1)

            def transpose_q(u):
                if not live(u):
                    return
                pe.wait_ge(qk_done[0], count(u))
                pe.wait_ge(qk_done[1], count(u))
                if begun(u, 2):
                    pe.wait_ge(yb_done, count(u, 2))
                for t in range(TPU):
                    last = nc.tensor.transpose(p_qT[:, t * P:(t + 1) * P], qk_tile(u, 0, t), ident[:])
                last.then_inc(qT_filled, 1)

            def key_value(u):
                if not live(u):
                    return
                if begun(u, 1):
                    pe.wait_ge(t1_done, count(u, 1))
                for t in range(TPU):
                    last = nc.tensor.matmul(p_kv[:, t // TPB, 0:D + 1], qk_tile(u, 1, t), gv[:, u.r, t, D:2 * D + 1],
                                            start=(t % TPB == 0), stop=(t % TPB == TPB - 1))
                last.then_inc(kv_filled, 1)

            def transpose_h2(u):
                if not live(u):
                    return
                s = u.r % 2
                pe.wait_ge(h2_done, count(u))
                pe.wait_ge(qT_done, count(u, -1))
                for t in range(TPU):
                    last = nc.tensor.transpose(p_h2T[:, t * P:(t + 1) * P], h2[:, s, t], identb[:])
                last.then_inc(h2T_filled, 1)

            def vsum_rows(u):
                if not live(u):
                    return
                s = u.r % 2
                pe.wait_ge(vsp_done, count(u))
                pe.wait_ge(rope_done[0], count(u))
                nc.tensor.matmul(p_vrow, vsp[:, s].rearrange("p j c -> p (j c)"), identb[:], start=True,
                                 stop=True).then_inc(vrow_filled, 1)

            def project_h(u, j):
                if not live(u):
                    return
                s = u.r % 2
                pe.wait_ge(hT_done, count(u))
                if begun(u, 1):
                    pe.wait_ge(rope_done[j], count(u, 1))
                if j == 0 and begun(u, 1):
                    pe.wait_ge(tap0_done, count(u, 1))
                    pe.wait_ge(vrow_done, count(u, 1))
                for a in range(TPB):
                    t = TPB * j + a
                    last_qk = nc.tensor.matmul(p_qk[j][:, a].rearrange("p h d -> p (h d)"),
                                               hT[:, s, t * P:(t + 1) * P],
                                               w_qk[:].rearrange("p a q d -> p (a q d)"), start=True, stop=True)
                    last_gv = nc.tensor.matmul(p_gv[j][:, a], hT[:, s, t * P:(t + 1) * P],
                                               w_gv[:].rearrange("p g d -> p (g d)"), start=True, stop=True)
                last_qk.then_inc(qk_filled[j], 1)
                last_gv.then_inc(gv_filled[j], 1)

            def transpose_o(u):
                if not live(u):
                    return
                s = u.r % 2
                pe.wait_ge(o_done, count(u))
                for t in range(TPU):
                    last = nc.tensor.transpose(p_oT[:, t * P:(t + 1) * P], o[:, s, t], ident[:])
                last.then_inc(oT_filled, 1)

            def ffn(u):
                if not live(u):
                    return
                s = u.r % 2
                pe.wait_ge(q8_done, count(u))
                pe.nop(nofuse=True)

                def products(q):
                    for t in range(TPU):
                        last = nc.tensor.matmul(p_y[:, t * P:(t + 1) * P], q[:, t * P:(t + 1) * P], fwq[:],
                                                start=True, stop=True)
                    last.then_inc(y_filled, 1)

                with pe.If(is_small == 1):
                    products(q8[:, s])
                with pe.If(is_small == 0):
                    products(q16)

            def project_o(u):
                if not live(u):
                    return
                s = u.r % 2
                pe.wait_ge(oT_done, count(u))
                pe.wait_ge(t1_done, count(u))
                for t in range(TPU):
                    last = nc.tensor.matmul(p_proj[:, t], oT[:, s, t * P:(t + 1) * P], w_o[:], start=True, stop=True)
                last.then_inc(proj_filled, 1)

            def step(t):
                project_h(unit(t, 1), 0)
                transpose_o(unit(t, 2))
                project_h(unit(t, 1), 1)
                project_o(unit(t, 2))
                transpose_v(unit(t, 1))
                transpose_q(unit(t, 1))
                key_value(unit(t, 1))
                vsum_rows(unit(t, 1))
                attend(unit(t, 1))
                transpose_h2(unit(t, 2))
                transpose_lepe(unit(t, 1))
                ffn(unit(t, 2))
                transpose_h(unit(t, 0))

            run_steps(pe, step)


N_LOADS = 18
N_ROUNDING = 9
SMALL = 21.0
_INS = ["L0_attn_hidden_states", "L0_attn_Wq", "L0_attn_Wk", "L0_attn_Wv", "L0_attn_Wg", "L0_attn_Wo",
        "L0_attn_lepe_w", "L0_attn_lepe_b", "L0_ffn_kernel", "L0_ffn_input_scale", "L0_ffn_kernel_scale",
        "L0_ffn_bias"]


def shape_constants():
    import numpy as np
    f32 = np.float32
    inv = (1.0 / np.float32(ROPE_BASE) ** (np.arange(0, DK, 2, dtype=f32) / np.float32(DK))).astype(f32)
    ang = np.arange(S, dtype=f32)[:, None] * inv[None, :]
    tab = ang.reshape(TPB, P, 1, HALF).transpose(1, 0, 2, 3)
    tab = np.broadcast_to(tab, (P, TPB, 2 * H, HALF)).reshape(P, TPB, D)
    cos, sin = np.cos(tab).astype(f32), np.sin(tab).astype(f32)
    cos_c = np.concatenate([cos, cos], axis=-1)
    sin_c = np.concatenate([-sin, sin], axis=-1)
    row_head = (np.arange(D) % (D // 2)) // HALF
    col_head = np.arange(D) // DK
    scale = f32(DK) ** f32(-0.5)
    mask = (row_head[:, None] == col_head[None, :]).astype(f32) * scale
    hmask = (row_head[:, None] == np.arange(H)[None, :]).astype(f32) * scale
    sel = np.repeat((np.arange(3 * BPU)[:, None] // 3 == np.arange(BPU)[None, :])[:, :, None], P, 2)
    vrow = np.zeros((3 * BPU, NW), f32)
    vrow[::3, D:] = S
    return {"cos": cos_c, "sin": sin_c, "ident": np.eye(P, dtype=f32),
            "mask": mask, "hmask": hmask, "sel": sel.astype(f32), "vrow": vrow}


def kernel(**inputs):
    import numpy as _np
    import concourse.bacc as _bacc
    from concourse import mybir as _mybir
    from concourse.bass_utils import run_bass_kernel_spmd as _run

    nc = _bacc.Bacc("TRN2", target_bir_lowering=False, num_devices=1)
    arrays, args = {}, []
    named = [(n, _np.ascontiguousarray(inputs[n])) for n in _INS] + list(shape_constants().items())
    for name, a in named:
        arrays[f"in_{name}_dram"] = a
        args.append(nc.dram_tensor(f"in_{name}_dram", a.shape, _mybir.dt.from_np(a.dtype), kind="ExternalInput").ap())
    args.append(nc.dram_tensor("out_dram", (B, S, D), F32, kind="ExternalOutput").ap())
    build(nc, *args)
    r = _run(nc, [arrays], core_ids=[0])
    return r.results[0]["out_dram"]
```

```python
from collections import namedtuple
from contextlib import ExitStack

import concourse.bass as bass
from concourse import mybir

P = 128
D = 128
B, S = 32, 256
H, DK = 8, 16
HALF = DK // 2
TAPS = 5
EPS = 1e-5
ROPE_BASE = 10000.0

TPB = S // P
BPU = 2
TPU = TPB * BPU
U = B // BPU
W = TPU * P
DEN = H
NW = D + DEN
LAG = 4
UNROLL = 4

F32 = mybir.dt.float32
BF16 = mybir.dt.bfloat16
F8 = mybir.dt.float8e4
I32 = mybir.dt.int32
ALU = mybir.AluOpType
ACT = mybir.ActivationFunctionType


Unit = namedtuple("Unit", "n r")


def unit(step, back):
    return Unit(step.n - back, (step.r - back) % UNROLL)


def live(u):
    return not isinstance(u.n, int) or 0 <= u.n < U


def reach(k):
    off = k - TAPS // 2
    return max(0, -off), min(S, S - off)


def begun(u, back):
    return not isinstance(u.n, int) or u.n >= back


def count(u, back=0):
    n = u.n - back
    return min(n, U - 1) + 1 if isinstance(n, int) else n + 1


def run_later_steps(eng, step):
    with eng.Fori(UNROLL, U, UNROLL) as i:
        for k in range(UNROLL):
            step(Unit(i + k, k))
    for t in range(U, U + LAG):
        step(Unit(t, t % UNROLL))


def build(nc, x, wq, wk, wv, wg, wo, lepe_w, lepe_b, ffn_w, s_in, s_k, ffn_b,
          cos_c, sin_c, ident_c, mask_c, hmask_c, sel_c, vrow_c, out):
    ctx = ExitStack()
    with ctx:
        def sb(name, shape, dt=F32):
            return ctx.enter_context(nc.sbuf_tensor(name, shape, dt))

        def ps(name, shape):
            return ctx.enter_context(nc.psum_tensor(name, shape, F32))

        def sem(name):
            return ctx.enter_context(nc.semaphore(name))

        cos_t = sb("cos_t", [P, TPB, 2 * D])
        sin_t = sb("sin_t", [P, TPB, 2 * D])
        ident = sb("ident", [P, P])
        identb = sb("identb", [P, P], BF16)
        mask = sb("mask", [P, D])
        hmask = sb("hmask", [P, H])
        sel = sb("sel", [3 * BPU, BPU, P], BF16)
        sel_f = sb("sel_f", [3 * BPU, BPU, P])
        vrow_f = sb("vrow_f", [3 * BPU, NW])
        w_raw = sb("w_raw", [P, 5, D])
        w_qk = sb("w_qk", [P, 2, 2, D // 2])
        w_gv = sb("w_gv", [P, 2, D])
        w_o = sb("w_o", [P, D])
        conv_w = sb("conv_w", [P, TAPS])
        conv_b = sb("conv_b", [P, 1])
        fw = sb("fw", [P, D], BF16)
        fwq = sb("fwq", [P, D], BF16)
        fb = sb("fb", [P, D], BF16)
        sc = sb("sc", [P, 2])
        rsc = sb("rsc", [P, 2])
        ysc = sb("ysc", [P, 1])
        small = sb("small", [P, 2], I32)
        qv = sb("qv", [P, W])
        qe = sb("qe", [P, W])
        qr = sb("qr", [P, W])
        qn = sb("qn", [P, W])
        minus_half = sb("minus_half", [P, TPU])
        scratch = sb("scratch", [P, 1])

        xs = sb("xs", [P, UNROLL, TPU, D])
        st1 = sb("st1", [P, 2, TPU, 6])
        mv1 = sb("mv1", [P, 2, TPU, 2])
        ve1 = sb("ve1", [P, 2, TPU])
        rs1 = sb("rs1", [P, 2, TPU])
        nmr1 = sb("nmr1", [P, 2, TPU])
        h = sb("h", [P, 2, TPU, D])
        hT = sb("hT", [P, 2, W])
        rc = sb("rc", [P, BPU, TPB, 2, D])
        rs = sb("rs", [P, BPU, TPB, 2, D])
        qk = sb("qk", [P, 2, BPU, 2, TPB * 2, D // 2])
        gv = sb("gv", [P, UNROLL, TPU, 2 * D + 1])
        qT = sb("qT", [P, 2, W])
        vT = sb("vT", [P, 2, BPU, S])
        vsum = sb("vsum", [P, 2, BPU])
        vres = sb("vres", [P, 2, BPU])
        vsp = sb("vsp", [P, 2, BPU, 3], BF16)
        vrow = sb("vrow", [3 * BPU, 2, NW], BF16)
        kvs = sb("kvs", [P, 2, BPU, NW])
        acc = sb("acc", [P, 2, BPU, S])
        outer = sb("outer", [P, 2, len(OUTER), BPU, S])
        rden = sb("rden", [P, TPU, H])
        t1 = sb("t1", [P, TPU, D])
        t2 = sb("t2", [P, 2, TPU, D])
        o = sb("o", [P, 2, TPU, D])
        oT = sb("oT", [P, 2, W])
        x2 = sb("x2", [P, 2, TPU, D])
        st2 = sb("st2", [P, 2, TPU, 6])
        mv2 = sb("mv2", [P, 2, TPU, 2])
        ve2 = sb("ve2", [P, 2, TPU])
        rs2 = sb("rs2", [P, 2, TPU])
        nmr2 = sb("nmr2", [P, 2, TPU])
        h2 = sb("h2", [P, 2, TPU, D], BF16)
        q8 = sb("q8", [P, 2, W], F8)
        q16 = sb("q16", [P, W], BF16)
        yb = sb("yb", [P, 2, TPU, D], BF16)
        yc = sb("yc", [P, 2, TPU, D], BF16)
        ob = sb("ob", [P, 2, TPU, D])

        p_qk = [ps(f"p_qk{j}", [P, TPB, 2, D]) for j in range(BPU)]
        p_gv = [ps(f"p_gv{j}", [P, TPB, 2 * D]) for j in range(BPU)]
        p_num = ps("p_num", [P, TPU, 2 * D])
        p_lepe = ps("p_lepe", [P, TPU, D])
        p_t = ps("p_t", [P, W])
        p_vT = p_gv[0][:, :, :].rearrange("p a d -> p (a d)").rearrange("p (j s) -> p j s", j=BPU)
        p_vrow = p_qk[0][0:3 * BPU, 0, 0, :]
        p_hT = p_gv[1][:, :, :].rearrange("p a d -> p (a d)")
        p_oT = p_lepe[:, :, :].rearrange("p t d -> p (t d)")
        p_qT, p_y = p_t, p_t
        p_kv = p_num[:, 0:2, :]
        p_proj = p_num[:, 2:4, :].rearrange("p t d -> p (t d)").rearrange("p (t d) -> p t d", t=TPU)
        p_h2T = p_t[:, 0:W // 2].bitcast(BF16)

        x_in = [sem(f"x_in{r}") for r in range(UNROLL)]
        w_in = sem("w_in")
        rope_in = sem("rope_in")
        c_in = sem("c_in")
        ob_free = [sem(f"ob_free{r}") for r in range(2)]
        setup_pe = sem("setup_pe")
        setup_dve = sem("setup_dve")
        w_ready = sem("w_ready")
        proj_ready = sem("proj_ready")
        rounding = [sem(f"rounding{n}") for n in range(N_ROUNDING)]
        w_chain = sem("w_chain")
        const_set = sem("const_set")
        bf16_ready = sem("bf16_ready")
        stats1_done = sem("stats1_done")
        aggr1_done = sem("aggr1_done")
        ve1_done = sem("ve1_done")
        pow1_done = sem("pow1_done")
        nmr1_done = sem("nmr1_done")
        h_done = sem("h_done")
        hT_filled = sem("hT_filled")
        hT_done = sem("hT_done")
        qk_filled = [sem(f"qk_filled{j}") for j in range(BPU)]
        gv_filled = [sem(f"gv_filled{j}") for j in range(BPU)]
        gv_done = [sem(f"gv_done{j}") for j in range(BPU)]
        rope_done = [sem(f"rope_done{j}") for j in range(BPU)]
        qk_done = [sem(f"qk_done{j}") for j in range(BPU)]
        vT_filled = sem("vT_filled")
        vT_done = sem("vT_done")
        tap0_done = sem("tap0_done")
        conv_done = [sem(f"conv_done{n}") for n in range(len(INNER))]
        outer_done = [sem(f"outer_done{n}") for n in range(len(OUTER))]
        outer_added = [sem(f"outer_added{n}") for n in range(len(OUTER))]
        vsp1 = sem("vsp1")
        vsp2 = sem("vsp2")
        vsp_done = sem("vsp_done")
        vrow_filled = sem("vrow_filled")
        vrow_done = sem("vrow_done")
        qT_filled = sem("qT_filled")
        qT_done = sem("qT_done")
        kv_filled = sem("kv_filled")
        kvs_done = sem("kvs_done")
        num_filled = sem("num_filled")
        rden_done = sem("rden_done")
        t1_done = sem("t1_done")
        lepe_filled = sem("lepe_filled")
        t2_done = sem("t2_done")
        o_done = sem("o_done")
        oT_filled = sem("oT_filled")
        oT_done = sem("oT_done")
        proj_filled = sem("proj_filled")
        x2_done = sem("x2_done")
        stats2_done = sem("stats2_done")
        aggr2_done = sem("aggr2_done")
        ve2_done = sem("ve2_done")
        pow2_done = sem("pow2_done")
        nmr2_done = sem("nmr2_done")
        h2_done = sem("h2_done")
        h2T_filled = sem("h2T_filled")
        q8_done = sem("q8_done")
        y_filled = sem("y_filled")
        yb_done = sem("yb_done")
        yc_done = sem("yc_done")
        ob_done = sem("ob_done")

        x_v = x.rearrange("(u j) (a p) d -> u p (j a) d", j=BPU, p=P)
        out_v = out.rearrange("(u j) (a p) d -> u p (j a) d", j=BPU, p=P)
        block = ctx.enter_context(nc.Block())

        @block.sync
        def _(sp):
            def load_x(u):
                if begun(u, UNROLL):
                    sp.wait_ge(x2_done, count(u, UNROLL))
                sp.dma_start(xs[:, u.r], x_v[u.n]).then_inc(x_in[u.r], 16)

            def store(u):
                if not live(u):
                    return
                sp.wait_ge(ob_done, count(u))
                sp.dma_start(out_v[u.n], ob[:, u.r % 2]).then_inc(ob_free[u.r % 2], 16)

            def step(t):
                if live(unit(t, -1)):
                    load_x(unit(t, -1))
                if live(unit(t, 4)):
                    store(unit(t, 4))

            load_x(Unit(0, 0))
            sp.dma_start(ident[:], ident_c).then_inc(w_in, 16)
            sp.dma_start(w_raw[:, 4], wo).then_inc(w_in, 16)
            for dst, src in ((cos_t[:], cos_c), (sin_t[:], sin_c)):
                sp.dma_start(dst, src).then_inc(rope_in, 16)
            load_x(Unit(1, 1))
            for dst, src in ((conv_w[:], lepe_w.rearrange("c a k -> c (a k)")),
                             (conv_b[:], lepe_b.rearrange("(c a) -> c a", a=1)),
                             (mask[:], mask_c), (hmask[:], hmask_c), (sel_f[:], sel_c), (vrow_f[:], vrow_c),
                             (fw[:], ffn_w),
                             (fb[:], ffn_b.rearrange("(a c) -> a c", a=1).broadcast_to([P, D])),
                             (sc[:, 0:1], s_in.rearrange("(a c) -> a c", a=1).broadcast_to([P, 1])),
                             (sc[:, 1:2], s_k.rearrange("(a c) -> a c", a=1).broadcast_to([P, 1]))):
                sp.dma_start(dst, src).then_inc(c_in, 16)

            for t in range(1, UNROLL):
                step(Unit(t, t))
            with sp.Fori(UNROLL, U - UNROLL, UNROLL) as i:
                for k in range(UNROLL):
                    step(Unit(i + k, k))
            for t in range(U - UNROLL, U + LAG):
                step(Unit(t, t % UNROLL))
            for r in range(2):
                sp.wait_ge(ob_free[r], 16 + 16 * (U // 2))

        @block.scalar
        def _(act):
            for n, w in enumerate((wq, wk, wv, wg)):
                act.dma_start(w_raw[:, n], w).then_inc(w_in, 16)
            act.wait_ge(const_set, 1)
            nc.scalar.activation(scratch[:], minus_half[:, 0:1], ACT.Identity)

            def quantise(u):
                act.wait_ge(h2T_filled, count(u))
                act.nop(nofuse=True)
                nc.scalar.activation(q8[:, u.r % 2], p_h2T, ACT.Copy, scale=rsc[:, 0:1],
                                     saturate=False).then_inc(q8_done, 1)

            def norm1(u):
                if not live(u):
                    return
                s = u.r % 2
                act.wait_ge(nmr1_done, count(u))
                if begun(u, 2):
                    act.wait_ge(hT_filled, count(u, 2))
                for t in range(TPU):
                    last = nc.scalar.activation(h[:, s, t], xs[:, u.r, t], ACT.Identity, scale=rs1[:, s, t:t + 1],
                                                bias=nmr1[:, s, t:t + 1])
                last.then_inc(h_done, 1)

            def norm2(u):
                if not live(u):
                    return
                s = u.r % 2
                act.wait_ge(nmr2_done, count(u))
                for t in range(TPU):
                    last = nc.scalar.activation(h2[:, s, t], x2[:, s, t], ACT.Identity, scale=rs2[:, s, t:t + 1],
                                                bias=nmr2[:, s, t:t + 1])
                last.then_inc(h2_done, 1)

            def quantise_if_small(u):
                if not live(u):
                    return
                with act.If(is_small == 1):
                    quantise(u)

            def move_vT(u):
                if not live(u):
                    return
                act.wait_ge(vT_filled, count(u))
                if begun(u, 2):
                    act.wait_ge(vsp_done, count(u, 2))
                    act.wait_ge(conv_done[-1], count(u, 2))
                for j in range(BPU):
                    last = nc.scalar.activation(vT[:, u.r % 2, j], p_vT[:, j], ACT.Copy,
                                                accum_out=vsum[:, u.r % 2, j:j + 1])
                last.then_inc(vT_done, 1)

            def conv_middle(u):
                if not live(u):
                    return
                act.wait_ge(vT_filled, count(u))
                if not begun(u, 1):
                    act.wait_ge(c_in, 16 * N_LOADS)
                if begun(u, 2):
                    act.wait_ge(lepe_filled, count(u, 2))
                nc.scalar.activation(acc[:, u.r % 2], p_vT, ACT.Identity, scale=conv_w[:, TAPS // 2:TAPS // 2 + 1],
                                     bias=conv_b[:, 0:1]).then_inc(tap0_done, 1)

            def conv_outer(u, n):
                if not live(u):
                    return
                k = OUTER[n]
                lo, hi = reach(k)
                off = k - TAPS // 2
                act.wait_ge(vT_done, count(u))
                if begun(u, 2):
                    act.wait_ge(outer_added[n], count(u, 2))
                nc.scalar.activation(outer[:, u.r % 2, n, :, lo:hi], vT[:, u.r % 2, :, lo + off:hi + off], ACT.Copy,
                                     scale=conv_w[:, k:k + 1]).then_inc(outer_done[n], 1)

            def move_y(u):
                if not live(u):
                    return
                act.wait_ge(y_filled, count(u))
                nc.scalar.activation(yb[:, u.r % 2], p_y[:].rearrange("p (t d) -> p t d", t=TPU), ACT.Copy,
                                     scale=ysc[:, 0:1]).then_inc(yb_done, 1)

            def move_qT(u):
                if not live(u):
                    return
                act.wait_ge(qT_filled, count(u))
                if begun(u, 2):
                    act.wait_ge(num_filled, count(u, 2))
                nc.scalar.activation(qT[:, u.r % 2], p_qT[:], ACT.Copy).then_inc(qT_done, 1)

            def move_vrow(u):
                if not live(u):
                    return
                act.wait_ge(vrow_filled, count(u))
                if begun(u, 2):
                    act.wait_ge(num_filled, count(u, 2))
                nc.scalar.activation(vrow[:, u.r % 2, 0:D], p_vrow, ACT.Copy).then_inc(vrow_done, 1)

            def move_oT(u):
                if not live(u):
                    return
                act.wait_ge(oT_filled, count(u))
                if begun(u, 1):
                    act.wait_ge(proj_filled, count(u, 1))
                nc.scalar.activation(oT[:, u.r % 2], p_oT, ACT.Copy).then_inc(oT_done, 1)

            def move_hT(u):
                if not live(u):
                    return
                act.wait_ge(hT_filled, count(u))
                if begun(u, 2):
                    act.wait_ge(gv_filled[-1], count(u, 2))
                nc.scalar.activation(hT[:, u.r % 2], p_hT, ACT.Copy).then_inc(hT_done, 1)

            def move_gv(u, j):
                if not live(u):
                    return
                act.wait_ge(gv_filled[j], count(u))
                if begun(u, 3):
                    act.wait_ge(o_done, count(u, 3))
                nc.scalar.activation(gv[:, u.r, TPB * j:TPB * (j + 1), 0:2 * D], p_gv[j][:],
                                     ACT.Copy).then_inc(gv_done[j], 1)

            def step(t):
                move_vT(unit(t, 2))
                conv_outer(unit(t, 2), 0)
                conv_outer(unit(t, 2), 1)
                norm2(unit(t, 4))
                move_gv(unit(t, 1), 1)
                quantise_if_small(unit(t, 4))
                move_oT(unit(t, 3))
                move_gv(unit(t, 1), 0)
                move_y(unit(t, 4))
                norm1(unit(t, 0))
                move_qT(unit(t, 2))
                move_vrow(unit(t, 2))
                conv_middle(unit(t, 1))
                move_hT(unit(t, 0))

            step(Unit(0, 0))
            step(Unit(1, 1))
            step(Unit(2, 2))
            step(Unit(3, 3))
            act.wait_ge(w_ready, 1)
            is_small = act.value_load(small[0:1, 0:1], min_val=0, max_val=1)
            run_later_steps(act, step)

        @block.gpsimd
        def _(pool):
            nc.gpsimd.memset(minus_half[:], -0.5)
            for r in range(2):
                nc.gpsimd.memset(ob[:, r, 0, 0:1], 0.0).then_inc(ob_free[r], 16)
            nc.gpsimd.memset(gv[:, :, :, 2 * D:2 * D + 1], 1.0).then_inc(const_set, 1)
            pool.wait_ge(const_set, 1)

            def add_rope(u, j):
                if not live(u):
                    return
                pool.wait_ge(rope_done[j], count(u))
                if begun(u, 2):
                    pool.wait_ge(kv_filled, count(u, 2))
                nc.gpsimd.tensor_tensor(
                    qk[:, u.r % 2, j].rearrange("p q t d -> p t q d"),
                    rc[:, j].rearrange("p a h (q d) -> p (a h) q d", q=2),
                    rs[:, j].rearrange("p a h (q d) -> p (a h) q d", q=2), ALU.add).then_inc(qk_done[j], 1)

            def gate(u):
                if not live(u):
                    return
                pool.wait_ge(t2_done, count(u))
                if begun(u, 2):
                    pool.wait_ge(oT_filled, count(u, 2))
                nc.gpsimd.tensor_tensor(o[:, u.r % 2], t2[:, u.r % 2], gv[:, u.r, :, 0:D],
                                        ALU.mult).then_inc(o_done, 1)

            def split_vsum(u):
                if not live(u):
                    return
                s = u.r % 2
                pool.wait_ge(vT_done, count(u))
                if begun(u, 2):
                    pool.wait_ge(vrow_filled, count(u, 2))
                pool.nop(nofuse=True)
                nc.gpsimd.tensor_scalar(vsp[:, s, :, 0], vsum[:, s], 1.0, 0.0, ALU.mult,
                                        ALU.add).then_inc(vsp1, 1)
                pool.wait_ge(vsp1, count(u))
                nc.gpsimd.tensor_tensor(vres[:, s], vsum[:, s], vsp[:, s, :, 0], ALU.subtract)
                nc.gpsimd.tensor_tensor(vsp[:, s, :, 1], vsum[:, s], vsp[:, s, :, 0],
                                        ALU.subtract).then_inc(vsp2, 1)
                pool.wait_ge(vsp2, count(u))
                nc.gpsimd.tensor_tensor(vsp[:, s, :, 2], vres[:, s], vsp[:, s, :, 1],
                                        ALU.subtract).then_inc(vsp_done, 1)

            def pow1(u):
                if not live(u):
                    return
                s = u.r % 2
                pool.wait_ge(ve1_done, count(u))
                if begun(u, 2):
                    pool.wait_ge(h_done, count(u, 2))
                nc.gpsimd.tensor_tensor(rs1[:, s], ve1[:, s], minus_half[:], ALU.pow).then_inc(pow1_done, 1)

            def pow2(u):
                if not live(u):
                    return
                s = u.r % 2
                pool.wait_ge(ve2_done, count(u))
                if begun(u, 1):
                    pool.wait_ge(h2_done, count(u, 1))
                nc.gpsimd.tensor_tensor(rs2[:, s], ve2[:, s], minus_half[:], ALU.pow).then_inc(pow2_done, 1)

            def sum_outer(u, n):
                if not live(u):
                    return
                s = u.r % 2
                pool.wait_ge(outer_done[n], count(u))
                if n == 0:
                    pool.wait_ge(conv_done[-1], count(u))
                else:
                    pool.wait_ge(outer_added[n - 1], count(u))
                lo, hi = reach(OUTER[n])
                part = acc[:, s, :, lo:hi]
                nc.gpsimd.tensor_tensor(part, part, outer[:, s, n, :, lo:hi], ALU.add).then_inc(outer_added[n], 1)

            def final_sum(u):
                if not live(u):
                    return
                s = u.r % 2
                pool.wait_ge(yc_done, count(u))
                pool.wait_ge(ob_free[s], (u.n - s) * 8 + 16)
                nc.gpsimd.tensor_tensor(ob[:, s], x2[:, s], yc[:, s], ALU.add).then_inc(ob_done, 1)

            def step(t):
                split_vsum(unit(t, 2))
                pow1(unit(t, 0))
                sum_outer(unit(t, 2), 0)
                sum_outer(unit(t, 2), 1)
                add_rope(unit(t, 1), 0)
                add_rope(unit(t, 1), 1)
                pow2(unit(t, 3))
                final_sum(unit(t, 4))
                gate(unit(t, 2))

            for t in range(UNROLL):
                step(Unit(t, t))
            run_later_steps(pool, step)

        @block.vector
        def _(dve):
            links = [0]

            def link(ins):
                links[0] += 1
                ins.then_inc(w_chain, 1)
                dve.wait_ge(w_chain, links[0])

            def set_up_projections():
                dve.wait_ge(setup_pe, 1)
                pw = p_num[:, 0:2, :].rearrange("p t d -> p (t d)").rearrange("p (w d) -> p w d", w=4)
                for n in range(2):
                    nc.vector.tensor_copy(w_qk[:, :, n].rearrange("p a (h f) -> p a h f", h=H),
                                          pw[:, n].rearrange("p (h a f) -> p a h f", h=H, a=2))
                nc.vector.tensor_copy(w_gv[:, 0], pw[:, 3])
                nc.vector.tensor_copy(w_gv[:, 1], pw[:, 2])
                nc.vector.tensor_copy(w_o[:], p_num[:, 2, 0:D]).then_inc(proj_ready, 1)

            def set_up_attention():
                dve.wait_ge(c_in, 16 * N_LOADS)
                nc.vector.tensor_copy(sel[:], sel_f[:])
                for r in range(2):
                    nc.vector.tensor_copy(vrow[:, r], vrow_f[:])
                nc.vector.tensor_copy(identb[:], ident[:]).then_inc(bf16_ready, 1)

            def set_up_ffn():
                link(nc.vector.reciprocal(rsc[:], sc[:]))
                nc.vector.tensor_tensor(ysc[:], sc[:, 0:1], sc[:, 1:2], ALU.mult)
                link(nc.vector.tensor_tensor(qr[:, 0:1], rsc[:, 0:1], rsc[:, 0:1], ALU.mult))
                link(nc.vector.tensor_scalar(small[:, 0:1], qr[:, 0:1], SMALL ** 2, 1.0, ALU.is_le, ALU.mult))
                link(nc.vector.tensor_scalar(qv[:, 0:D], fw[:], rsc[:, 1:2], None, ALU.mult))
                round_e4m3fn(fwq[:], D, lambda n, ins: link(ins))
                nc.vector.tensor_copy(qe[:, 0:1], ysc[:]).then_inc(w_ready, 1)

            def round_e4m3fn(dst, cols, link_nth):
                v, e, r, n = (b[:, 0:cols] for b in (qv, qe, qr, qn))
                link_nth(0, nc.vector.tensor_scalar(e.bitcast(I32), v.bitcast(I32), 0x7F800000, None,
                                                    ALU.bitwise_and))
                link_nth(1, nc.vector.tensor_scalar(e, e, 2.0 ** -6, 1.5 * 2.0 ** 20, ALU.max, ALU.mult))
                link_nth(2, nc.vector.tensor_tensor(r, v, e, ALU.add))
                link_nth(3, nc.vector.tensor_tensor(r, r, e, ALU.subtract))
                link_nth(4, nc.vector.tensor_tensor(n, r, r, ALU.mult))
                link_nth(5, nc.vector.tensor_scalar(n, n, 448.0 ** 2, 3e38, ALU.is_gt, ALU.mult))
                link_nth(6, nc.vector.tensor_scalar(n, n, 3e38, 0.0, ALU.mult, ALU.mult))
                link_nth(7, nc.vector.tensor_tensor(dst, r, n, ALU.add))

            def quantise_if_wide(u):
                if not live(u):
                    return
                def link_nth(n, ins):
                    ins.then_inc(rounding[n], 1)
                    dve.wait_ge(rounding[n], count(u))
                    dve.nop(nofuse=True)

                with dve.If(is_small == 0):
                    dve.wait_ge(h2T_filled, count(u))
                    dve.nop(nofuse=True)
                    link_nth(8, nc.vector.tensor_scalar(qv[:], p_h2T, rsc[:, 0:1], None, ALU.mult))
                    round_e4m3fn(q16[:], W, link_nth)
                    nc.vector.tensor_copy(qe[:, 0:1], rsc[:, 0:1]).then_inc(q8_done, 1)

            def rope(u, j):
                if not live(u):
                    return
                dve.wait_ge(qk_filled[j], count(u))
                if begun(u, 1):
                    dve.wait_ge(qk_done[j], count(u, 1))
                nc.vector.tensor_tensor(rc[:, j], p_qk[j][:], cos_t[:].rearrange("p a (h d) -> p a h d", h=2),
                                        ALU.mult)
                nc.vector.tensor_tensor(rs[:, j], p_qk[j][:, :, ::-1, :],
                                        sin_t[:].rearrange("p a (h d) -> p a h d", h=2),
                                        ALU.mult).then_inc(rope_done[j], 1)

            def invert(u):
                if not live(u):
                    return
                dve.wait_ge(num_filled, count(u))
                nc.vector.reciprocal(rden[:], p_num[:, :, D:NW]).then_inc(rden_done, 1)

            def divide(u):
                if not live(u):
                    return
                dve.wait_ge(rden_done, count(u))
                nc.vector.tensor_tensor(t1[:].rearrange("p t (h e) -> p t h e", h=H),
                                        p_num[:, :, 0:D].rearrange("p t (h e) -> p t h e", h=H),
                                        rden[:].unsqueeze(3).to_broadcast([P, TPU, H, DK]),
                                        ALU.mult).then_inc(t1_done, 1)

            def add_lepe(u):
                if not live(u):
                    return
                dve.wait_ge(lepe_filled, count(u))
                dve.wait_ge(t1_done, count(u))
                if begun(u, 2):
                    dve.wait_ge(o_done, count(u, 2))
                nc.vector.tensor_tensor(t2[:, u.r % 2], t1[:], p_lepe[:], ALU.add).then_inc(t2_done, 1)

            def stats1(u):
                if not live(u):
                    return
                dve.wait_ge(x_in[u.r], (u.n - u.r) * (16 // UNROLL) + 16)
                for t in range(TPU):
                    last = nc.vector.bn_stats(st1[:, u.r % 2, t], xs[:, u.r, t])
                last.then_inc(stats1_done, 1)

            def mean_var1(u):
                if not live(u):
                    return
                s = u.r % 2
                dve.wait_ge(stats1_done, count(u))
                dve.nop(nofuse=True)
                for t in range(TPU):
                    last = nc.vector.bn_aggr(mv1[:, s, t], st1[:, s, t])
                last.then_inc(aggr1_done, 1)

            def var_eps1(u):
                if not live(u):
                    return
                s = u.r % 2
                dve.wait_ge(aggr1_done, count(u))
                dve.nop(nofuse=True)
                nc.vector.tensor_scalar(ve1[:, s], mv1[:, s, :, 1], 1.0, EPS, ALU.mult,
                                        ALU.add).then_inc(ve1_done, 1)

            def negate_mean1(u):
                if not live(u):
                    return
                s = u.r % 2
                dve.wait_ge(pow1_done, count(u))
                if begun(u, 2):
                    dve.wait_ge(h_done, count(u, 2))
                nc.vector.scalar_tensor_tensor(out=nmr1[:, s], in0=mv1[:, s, :, 0], scalar=-1.0, in1=rs1[:, s],
                                               op0=ALU.mult, op1=ALU.mult).then_inc(nmr1_done, 1)

            def stats2(u):
                if not live(u):
                    return
                dve.wait_ge(x2_done, count(u))
                for t in range(TPU):
                    last = nc.vector.bn_stats(st2[:, u.r % 2, t], x2[:, u.r % 2, t])
                last.then_inc(stats2_done, 1)

            def mean_var2(u):
                if not live(u):
                    return
                s = u.r % 2
                dve.wait_ge(stats2_done, count(u))
                dve.nop(nofuse=True)
                for t in range(TPU):
                    last = nc.vector.bn_aggr(mv2[:, s, t], st2[:, s, t])
                last.then_inc(aggr2_done, 1)

            def var_eps2(u):
                if not live(u):
                    return
                s = u.r % 2
                dve.wait_ge(aggr2_done, count(u))
                dve.nop(nofuse=True)
                nc.vector.tensor_scalar(ve2[:, s], mv2[:, s, :, 1], 1.0, EPS, ALU.mult,
                                        ALU.add).then_inc(ve2_done, 1)

            def negate_mean2(u):
                if not live(u):
                    return
                s = u.r % 2
                dve.wait_ge(pow2_done, count(u))
                nc.vector.scalar_tensor_tensor(out=nmr2[:, s], in0=mv2[:, s, :, 0], scalar=-1.0, in1=rs2[:, s],
                                               op0=ALU.mult, op1=ALU.mult).then_inc(nmr2_done, 1)

            def conv_inner(u, n):
                if not live(u):
                    return
                s = u.r % 2
                k = INNER[n]
                lo, hi = reach(k)
                off = k - TAPS // 2
                dve.wait_ge(vT_done, count(u))
                if n == 0:
                    dve.wait_ge(tap0_done, count(u))
                else:
                    dve.wait_ge(conv_done[0], count(u))
                part = acc[:, s, :, lo:hi]
                nc.vector.scalar_tensor_tensor(out=part, in0=vT[:, s, :, lo + off:hi + off],
                                               scalar=conv_w[:, k:k + 1], in1=part, op0=ALU.mult,
                                               op1=ALU.add).then_inc(conv_done[n], 1)

            def mask_kv(u):
                if not live(u):
                    return
                s = u.r % 2
                dve.wait_ge(kv_filled, count(u))
                if begun(u, 2):
                    dve.wait_ge(num_filled, count(u, 2))
                nc.vector.tensor_tensor(kvs[:, s, :, 0:D], p_kv[:, :, 0:D],
                                        mask[:].unsqueeze(1).to_broadcast([P, BPU, D]), ALU.mult)
                nc.vector.tensor_tensor(kvs[:, s, :, D:NW], p_kv[:, :, D:D + 1].to_broadcast([P, BPU, H]),
                                        hmask[:].unsqueeze(1).to_broadcast([P, BPU, H]),
                                        ALU.mult).then_inc(kvs_done, 1)

            def residual(u):
                if not live(u):
                    return
                s = u.r % 2
                dve.wait_ge(proj_filled, count(u))
                nc.vector.tensor_tensor(x2[:, s], xs[:, u.r], p_proj, ALU.add).then_inc(x2_done, 1)

            def add_bias(u):
                if not live(u):
                    return
                s = u.r % 2
                dve.wait_ge(yb_done, count(u))
                nc.vector.tensor_tensor(yc[:, s], yb[:, s], fb[:].unsqueeze(1).to_broadcast([P, TPU, D]),
                                        ALU.add).then_inc(yc_done, 1)

            def step(t):
                stats1(unit(t, 0))
                conv_inner(unit(t, 2), 0)
                mean_var1(unit(t, 0))
                var_eps1(unit(t, 0))
                conv_inner(unit(t, 2), 1)
                rope(unit(t, 1), 1)
                negate_mean1(unit(t, 0))
                rope(unit(t, 1), 0)
                quantise_if_wide(unit(t, 4))
                residual(unit(t, 3))
                mask_kv(unit(t, 2))
                stats2(unit(t, 3))
                mean_var2(unit(t, 3))
                var_eps2(unit(t, 3))
                add_bias(unit(t, 4))
                invert(unit(t, 2))
                divide(unit(t, 2))
                negate_mean2(unit(t, 3))
                add_lepe(unit(t, 2))

            step(Unit(0, 0))
            set_up_projections()
            dve.wait_ge(rope_in, 32)
            step(Unit(1, 1))
            set_up_attention()
            set_up_ffn()
            step(Unit(2, 2))
            step(Unit(3, 3))
            dve.wait_ge(w_ready, 1)
            is_small = dve.value_load(small[0:1, 0:1], min_val=0, max_val=1)
            run_later_steps(dve, step)

        @block.tensor
        def _(pe):
            pe.wait_ge(w_in, 16 * 6)
            for n in range(4):
                nc.tensor.transpose(p_num[:, n // 2, (n % 2) * D:(n % 2 + 1) * D], w_raw[:, n], ident[:])
            nc.tensor.transpose(p_num[:, 2, 0:D], w_raw[:, 4], ident[:]).then_inc(setup_pe, 1)
            def qk_tile(u, q_or_k, t):
                a = t % TPB
                return qk[:, u.r % 2, t // TPB, q_or_k, 2 * a:2 * a + 2].rearrange("p h d -> p (h d)")

            def attend(u):
                if not live(u):
                    return
                s = u.r % 2
                pe.wait_ge(qT_done, count(u))
                pe.wait_ge(kvs_done, count(u))
                pe.wait_ge(vrow_done, count(u))
                if begun(u, 1):
                    pe.wait_ge(x2_done, count(u, 1))
                for t in range(TPU):
                    j = t // TPB
                    nc.tensor.matmul(p_num[:, t, 0:NW], qT[:, s, t * P:(t + 1) * P], kvs[:, s, j],
                                     start=True, stop=False)
                    last = nc.tensor.matmul(p_num[:, t, 0:NW], sel[:, j], vrow[:, s], start=False, stop=True)
                last.then_inc(num_filled, 1)

            def transpose_lepe(u):
                if not live(u):
                    return
                s = u.r % 2
                pe.wait_ge(outer_added[-1], count(u))
                if begun(u, 1):
                    pe.wait_ge(oT_done, count(u, 1))
                for t in range(TPU):
                    a = t % TPB
                    last = nc.tensor.transpose(p_lepe[:, t], acc[:, s, t // TPB, a * P:(a + 1) * P], ident[:])
                last.then_inc(lepe_filled, 1)

            def transpose_v(u):
                if not live(u):
                    return
                pe.wait_ge(gv_done[0], count(u))
                pe.wait_ge(gv_done[1], count(u))
                for t in range(TPU):
                    a = t % TPB
                    last = nc.tensor.transpose(p_vT[:, t // TPB, a * P:(a + 1) * P], gv[:, u.r, t, D:2 * D], ident[:])
                last.then_inc(vT_filled, 1)

            def transpose_h(u):
                if not live(u):
                    return
                s = u.r % 2
                pe.wait_ge(h_done, count(u))
                if begun(u, 1):
                    pe.wait_ge(gv_done[1], count(u, 1))
                for t in range(TPU):
                    last = nc.tensor.transpose(p_hT[:, t * P:(t + 1) * P], h[:, s, t], ident[:])
                last.then_inc(hT_filled, 1)

            def transpose_q(u):
                if not live(u):
                    return
                pe.wait_ge(qk_done[0], count(u))
                pe.wait_ge(qk_done[1], count(u))
                if begun(u, 2):
                    pe.wait_ge(yb_done, count(u, 2))
                for t in range(TPU):
                    last = nc.tensor.transpose(p_qT[:, t * P:(t + 1) * P], qk_tile(u, 0, t), ident[:])
                last.then_inc(qT_filled, 1)

            def key_value(u):
                if not live(u):
                    return
                pe.wait_ge(qk_done[0], count(u))
                pe.wait_ge(qk_done[1], count(u))
                if begun(u, 1):
                    pe.wait_ge(t1_done, count(u, 1))
                for t in range(TPU):
                    last = nc.tensor.matmul(p_kv[:, t // TPB, 0:D + 1], qk_tile(u, 1, t), gv[:, u.r, t, D:2 * D + 1],
                                            start=(t % TPB == 0), stop=(t % TPB == TPB - 1))
                last.then_inc(kv_filled, 1)

            def transpose_h2(u):
                if not live(u):
                    return
                s = u.r % 2
                pe.wait_ge(h2_done, count(u))
                pe.wait_ge(qT_done, count(u, -1))
                for t in range(TPU):
                    last = nc.tensor.transpose(p_h2T[:, t * P:(t + 1) * P], h2[:, s, t], identb[:])
                last.then_inc(h2T_filled, 1)

            def vsum_rows(u):
                if not live(u):
                    return
                s = u.r % 2
                pe.wait_ge(vsp_done, count(u))
                if not begun(u, 1):
                    pe.wait_ge(bf16_ready, 1)
                pe.wait_ge(rope_done[0], count(u, -1))
                nc.tensor.matmul(p_vrow, vsp[:, s].rearrange("p j c -> p (j c)"), identb[:], start=True,
                                 stop=True).then_inc(vrow_filled, 1)

            def project_h(u, j):
                if not live(u):
                    return
                s = u.r % 2
                pe.wait_ge(hT_done, count(u))
                if not begun(u, 1):
                    pe.wait_ge(proj_ready, 1)
                if begun(u, 1):
                    pe.wait_ge(rope_done[j], count(u, 1))
                if j == 0 and begun(u, 1):
                    pe.wait_ge(vT_done, count(u, 1))
                    pe.wait_ge(tap0_done, count(u, 1))
                if j == 0 and begun(u, 2):
                    pe.wait_ge(vrow_done, count(u, 2))
                for a in range(TPB):
                    t = TPB * j + a
                    last_qk = nc.tensor.matmul(p_qk[j][:, a].rearrange("p h d -> p (h d)"),
                                               hT[:, s, t * P:(t + 1) * P],
                                               w_qk[:].rearrange("p a q d -> p (a q d)"), start=True, stop=True)
                    last_gv = nc.tensor.matmul(p_gv[j][:, a], hT[:, s, t * P:(t + 1) * P],
                                               w_gv[:].rearrange("p g d -> p (g d)"), start=True, stop=True)
                last_qk.then_inc(qk_filled[j], 1)
                last_gv.then_inc(gv_filled[j], 1)

            def transpose_o(u):
                if not live(u):
                    return
                s = u.r % 2
                pe.wait_ge(o_done, count(u))
                for t in range(TPU):
                    last = nc.tensor.transpose(p_oT[:, t * P:(t + 1) * P], o[:, s, t], ident[:])
                last.then_inc(oT_filled, 1)

            def ffn(u):
                if not live(u):
                    return
                s = u.r % 2
                pe.wait_ge(q8_done, count(u))
                pe.nop(nofuse=True)

                def products(q):
                    for t in range(TPU):
                        last = nc.tensor.matmul(p_y[:, t * P:(t + 1) * P], q[:, t * P:(t + 1) * P], fwq[:],
                                                start=True, stop=True)
                    last.then_inc(y_filled, 1)

                with pe.If(is_small == 1):
                    products(q8[:, s])
                with pe.If(is_small == 0):
                    products(q16)

            def project_o(u):
                if not live(u):
                    return
                s = u.r % 2
                pe.wait_ge(oT_done, count(u))
                pe.wait_ge(t1_done, count(u))
                for t in range(TPU):
                    last = nc.tensor.matmul(p_proj[:, t], oT[:, s, t * P:(t + 1) * P], w_o[:], start=True, stop=True)
                last.then_inc(proj_filled, 1)

            def step(t):
                project_h(unit(t, 1), 0)
                transpose_h2(unit(t, 4))
                transpose_o(unit(t, 3))
                key_value(unit(t, 2))
                ffn(unit(t, 4))
                project_o(unit(t, 3))
                transpose_q(unit(t, 2))
                transpose_v(unit(t, 1))
                vsum_rows(unit(t, 2))
                transpose_lepe(unit(t, 2))
                transpose_h(unit(t, 0))
                attend(unit(t, 2))
                project_h(unit(t, 0), 1)

            step(Unit(0, 0))
            step(Unit(1, 1))
            pe.wait_ge(const_set, 1)
            step(Unit(2, 2))
            step(Unit(3, 3))
            pe.wait_ge(w_ready, 1)
            is_small = pe.value_load(small[0:1, 0:1], min_val=0, max_val=1)
            run_later_steps(pe, step)


N_LOADS = 10
INNER = (1, 3)
OUTER = (0, 4)
N_ROUNDING = 9
SMALL = 21.0
_INS = ["L0_attn_hidden_states", "L0_attn_Wq", "L0_attn_Wk", "L0_attn_Wv", "L0_attn_Wg", "L0_attn_Wo",
        "L0_attn_lepe_w", "L0_attn_lepe_b", "L0_ffn_kernel", "L0_ffn_input_scale", "L0_ffn_kernel_scale",
        "L0_ffn_bias"]


def shape_constants():
    import numpy as np
    f32 = np.float32
    inv = (1.0 / np.float32(ROPE_BASE) ** (np.arange(0, DK, 2, dtype=f32) / np.float32(DK))).astype(f32)
    ang = np.arange(S, dtype=f32)[:, None] * inv[None, :]
    tab = ang.reshape(TPB, P, 1, HALF).transpose(1, 0, 2, 3)
    tab = np.broadcast_to(tab, (P, TPB, 2 * H, HALF)).reshape(P, TPB, D)
    cos, sin = np.cos(tab).astype(f32), np.sin(tab).astype(f32)
    cos_c = np.concatenate([cos, cos], axis=-1)
    sin_c = np.concatenate([-sin, sin], axis=-1)
    row_head = (np.arange(D) % (D // 2)) // HALF
    col_head = np.arange(D) // DK
    scale = f32(DK) ** f32(-0.5)
    mask = (row_head[:, None] == col_head[None, :]).astype(f32) * scale
    hmask = (row_head[:, None] == np.arange(H)[None, :]).astype(f32) * scale
    sel = np.repeat((np.arange(3 * BPU)[:, None] // 3 == np.arange(BPU)[None, :])[:, :, None], P, 2)
    vrow = np.zeros((3 * BPU, NW), f32)
    vrow[::3, D:] = S
    return {"cos": cos_c, "sin": sin_c, "ident": np.eye(P, dtype=f32),
            "mask": mask, "hmask": hmask, "sel": sel.astype(f32), "vrow": vrow}


def kernel(**inputs):
    import numpy as _np
    import concourse.bacc as _bacc
    from concourse import mybir as _mybir
    from concourse.bass_utils import run_bass_kernel_spmd as _run

    nc = _bacc.Bacc("TRN2", target_bir_lowering=False, num_devices=1)
    arrays, args = {}, []
    named = [(n, _np.ascontiguousarray(inputs[n])) for n in _INS] + list(shape_constants().items())
    for name, a in named:
        arrays[f"in_{name}_dram"] = a
        args.append(nc.dram_tensor(f"in_{name}_dram", a.shape, _mybir.dt.from_np(a.dtype), kind="ExternalInput").ap())
    args.append(nc.dram_tensor("out_dram", (B, S, D), F32, kind="ExternalOutput").ap())
    build(nc, *args)
    r = _run(nc, [arrays], core_ids=[0])
    return r.results[0]["out_dram"]
```
